# Optimizing a Trainium2 kernel written in Bass

```python
import numpy as np
import jax
import jax.numpy as jnp

def _softmax(x, axis=-1):
    return jax.nn.softmax(x, axis=axis)

def _gelu(x):
    return jax.nn.gelu(x, approximate=True)

def _silu(x):
    return jax.nn.silu(x)

def _sigmoid(x):
    return jax.nn.sigmoid(x)

def _layernorm(x, axis=-1, eps=1e-05):
    m = jnp.mean(x, axis=axis, keepdims=True)
    v = jnp.var(x, axis=axis, keepdims=True)
    return (x - m) / jnp.sqrt(v + eps)

def _scatter_add(tgt, idx, src, axis=0):
    return tgt.at[idx].add(src)

def _segment_sum(src, seg, n):
    return jax.ops.segment_sum(src, seg, n)
kernel_name = 'mk_gnn_resnorm_d1_gnn_r8_228e2d'

def setup_inputs(seed: int=0):
    np.random.seed(seed)
    _w = jnp.asarray

    def _rec_inputs():
        import jax
        import jax.numpy as jnp
        _gk = jax.random.key(seed)
        x = -0.0002117 + 1 * jax.random.normal(jax.random.fold_in(_gk, 1), (12500, 256), jnp.float32)
        src = jax.random.randint(jax.random.fold_in(_gk, 2), (200000,), 0, 12500, jnp.int32)
        dst = jax.random.randint(jax.random.fold_in(_gk, 3), (200000,), 0, 12500, jnp.int32)
        _o = jnp.argsort(dst, stable=True)
        src = src[_o]
        dst = dst[_o]
        return (x, src, dst)
    x, src, dst = _rec_inputs()

    def _L0_gnn_setup():
        import jax, jax.numpy as jnp
        import numpy as np
        N_NODES = 12500
        N_EDGES = 200000
        NFEAT, NHID, NCLASS = (256, 512, 256)

        def _init_params(key):
            ks = jax.random.split(key, 8)
            s = 0.02
            p = {'W1a': jax.random.normal(ks[0], (NFEAT, NHID), jnp.float32) * s, 'b1a': jnp.zeros((NHID,), jnp.float32), 'W1b': jax.random.normal(ks[1], (NHID, NHID), jnp.float32) * s, 'b1b': jnp.zeros((NHID,), jnp.float32), 'W2a': jax.random.normal(ks[2], (NHID, NHID), jnp.float32) * s, 'b2a': jnp.zeros((NHID,), jnp.float32), 'W2b': jax.random.normal(ks[3], (NHID, NCLASS), jnp.float32) * s, 'b2b': jnp.zeros((NCLASS,), jnp.float32), 'eps1': jnp.zeros((), jnp.float32), 'eps2': jnp.zeros((), jnp.float32)}
            return p

        def _gin_agg(h, src, dst, eps, n_nodes):
            agg = jax.ops.segment_sum(h[src], dst, num_segments=n_nodes)
            return (1.0 + eps) * h + agg
        key = jax.random.key(seed)
        kx, ke, kp = jax.random.split(key, 3)
        x = jax.random.normal(kx, (N_NODES, NFEAT), jnp.float32)
        edge_index = jax.random.randint(ke, (2, N_EDGES), 0, N_NODES, jnp.int64)
        inp = {'x': x, 'edge_index': edge_index}
        inp.update(_init_params(kp))
        return inp
    _L0_gnn_all = _L0_gnn_setup()
    _L0_gnn_in = {k: v for k, v in _L0_gnn_all.items() if k in ('W1a', 'b1a', 'W1b', 'b1b', 'W2a', 'b2a', 'W2b', 'b2b', 'eps1', 'eps2')}
    del _L0_gnn_all
    return {'x': x, 'src': src, 'dst': dst, 'L0_gnn_W1a': _L0_gnn_in['W1a'], 'L0_gnn_b1a': _L0_gnn_in['b1a'], 'L0_gnn_W1b': _L0_gnn_in['W1b'], 'L0_gnn_b1b': _L0_gnn_in['b1b'], 'L0_gnn_W2a': _L0_gnn_in['W2a'], 'L0_gnn_b2a': _L0_gnn_in['b2a'], 'L0_gnn_W2b': _L0_gnn_in['W2b'], 'L0_gnn_b2b': _L0_gnn_in['b2b'], 'L0_gnn_eps1': _L0_gnn_in['eps1'], 'L0_gnn_eps2': _L0_gnn_in['eps2']}

def reference(x, src, dst, L0_gnn_W1a, L0_gnn_b1a, L0_gnn_W1b, L0_gnn_b1b, L0_gnn_W2a, L0_gnn_b2a, L0_gnn_W2b, L0_gnn_b2b, L0_gnn_eps1, L0_gnn_eps2):
    import jax
    import jax.numpy as jnp

    def _L0_gnn_ref(x, edge_index, W1a, b1a, W1b, b1b, W2a, b2a, W2b, b2b, eps1, eps2):
        import jax, jax.numpy as jnp
        import numpy as np
        N_NODES = 12500
        N_EDGES = 200000
        NFEAT, NHID, NCLASS = (256, 512, 256)

        def _init_params(key):
            ks = jax.random.split(key, 8)
            s = 0.02
            p = {'W1a': jax.random.normal(ks[0], (NFEAT, NHID), jnp.float32) * s, 'b1a': jnp.zeros((NHID,), jnp.float32), 'W1b': jax.random.normal(ks[1], (NHID, NHID), jnp.float32) * s, 'b1b': jnp.zeros((NHID,), jnp.float32), 'W2a': jax.random.normal(ks[2], (NHID, NHID), jnp.float32) * s, 'b2a': jnp.zeros((NHID,), jnp.float32), 'W2b': jax.random.normal(ks[3], (NHID, NCLASS), jnp.float32) * s, 'b2b': jnp.zeros((NCLASS,), jnp.float32), 'eps1': jnp.zeros((), jnp.float32), 'eps2': jnp.zeros((), jnp.float32)}
            return p

        def _gin_agg(h, src, dst, eps, n_nodes):
            agg = jax.ops.segment_sum(h[src], dst, num_segments=n_nodes)
            return (1.0 + eps) * h + agg
        src, dst = (edge_index[0], edge_index[1])
        n = x.shape[0]
        h = _gin_agg(x, src, dst, eps1, n)
        h = jax.nn.relu(h @ W1a + b1a)
        h = jax.nn.relu(h @ W1b + b1b)
        h = _gin_agg(h, src, dst, eps2, n)
        h = jax.nn.relu(h @ W2a + b2a)
        out = h @ W2b + b2b
        return out
    edge_index = jnp.stack([src, dst])
    x = _layernorm(x + _L0_gnn_ref(x, edge_index, L0_gnn_W1a, L0_gnn_b1a, L0_gnn_W1b, L0_gnn_b1b, L0_gnn_W2a, L0_gnn_b2a, L0_gnn_W2b, L0_gnn_b2b, L0_gnn_eps1, L0_gnn_eps2), axis=-1)
    return x

_drawn_inputs = setup_inputs


def setup_inputs(seed=0):
    import zlib

    import numpy as np

    out = dict(_drawn_inputs(seed))
    spreads = {'L0_gnn_b1a': (0.0, 0.291),
     'L0_gnn_b1b': (0.0, 0.1),
     'L0_gnn_b2a': (0.0, 0.282),
     'L0_gnn_b2b': (0.0, 0.1)}
    factors = {}
    for name, (base, spread) in spreads.items():
        noise = np.random.default_rng([zlib.crc32(name.encode()), seed]).standard_normal(out[name].shape)
        drawn = base * np.exp(spread * noise) if base else spread * noise
        out[name] = jnp.asarray(drawn.astype(out[name].dtype))
    for name, factor in factors.items():
        out[name] = (out[name] * factor).astype(out[name].dtype)
    return out
```

```python
import concourse.bass as bass
from concourse import mybir
from contextlib import ExitStack

F32 = mybir.dt.float32
I32 = mybir.dt.int32
ALU = mybir.AluOpType
ACT = mybir.ActivationFunctionType
AX_X = mybir.AxisListType.X

N_NODES, N_EDGES = 12500, 200000
F_IN, F_HID, F_OUT = 256, 512, 256
P = 128
NODES_W = 125
WINS = 4
ROUNDS = N_NODES // (NODES_W * WINS)
N_WIN = ROUNDS * WINS
NODES_R = NODES_W * WINS
TILES = 17
ROOM = TILES * P
GROUPS = [(0, 4), (4, 8), (8, 12), (12, TILES)]
NG = len(GROUPS)
RING = 2 * TILES
PAD_NODE = 1 << 23
SAMPLE = 500
N_SAMP = N_EDGES // SAMPLE
N_BND = N_WIN + 1
SORT_P = 125
SORT_F = N_EDGES // SORT_P
GEN_E = 125
GEN_TILES = N_EDGES // GEN_E
KA = [F_IN // P, F_HID // P]
MB = F_HID // P
F_TAB = [F_IN, F_HID]
F_RES = [F_HID, F_OUT]
LN_EPS = 1e-5


def build(nc, x, src, dst, w1a, b1a, w1b, b1b, w2a, b2a, w2b, b2b, eps1, eps2, out):
    ctx = ExitStack()
    with ctx:
        def sb(name, shape, dt=F32):
            return ctx.enter_context(nc.sbuf_tensor(name, shape, dt))

        def sem(name):
            return ctx.enter_context(nc.semaphore(name))

        def scratch(name, shape, dt=F32):
            return nc.dram_tensor(name, shape, dt, kind="Internal").ap()

        hidden = scratch("hidden", [N_NODES, F_HID])
        src_pad = scratch("src_pad", [N_EDGES + ROOM], I32)
        dst_pad = scratch("dst_pad", [N_EDGES + ROOM], I32)
        samples_dram = scratch("samples_dram", [N_SAMP], I32)
        base_table = [scratch("base_table1", [N_NODES, F_IN]), scratch("base_table2", [N_NODES, F_HID])]
        table = [x, hidden]
        result = [hidden, out]

        rows = sb("rows", [P, RING, F_HID])
        onehot = sb("onehot", [P, 2, TILES, NODES_W])
        src_idx = sb("src_idx", [P, WINS, TILES], I32)
        dst_idx = sb("dst_idx", [P, WINS, TILES], I32)
        node_ids = sb("node_ids", [P, NODES_W])
        ids_over = sb("ids_over", [P, NODES_W])
        own = sb("own", [NODES_W, WINS, F_HID])
        z = sb("z", [NODES_W, WINS, F_HID])
        zT = sb("zT", [P, MB, NODES_R])
        aT = sb("aT", [P, MB, NODES_R])
        staged = sb("staged", [NODES_W, WINS, F_HID])
        resid = sb("resid", [NODES_W, WINS, F_OUT])
        wa = [sb("wa1", [P, KA[0], F_HID]), sb("wa2", [P, KA[1], F_HID])]
        wb = [sb("wb1", [P, MB, F_HID]), sb("wb2", [P, MB, F_OUT])]
        ba = [sb("ba1", [P, MB]), sb("ba2", [P, MB])]
        bb = [sb("bb1", [NODES_W, F_HID]), sb("bb2", [NODES_W, F_OUT])]
        ident = sb("ident", [P, P])
        ones = sb("ones", [P, P])
        eps = sb("eps", [NODES_W, 2])
        own_scale = sb("own_scale", [NODES_W, 2])
        gen_scale = sb("gen_scale", [NODES_W, 2])
        stats = sb("stats", [NODES_W, 6])
        meanvar = sb("meanvar", [NODES_W, WINS, 2])
        var_eps, std, rstd, shift = (sb(n, [NODES_W, WINS]) for n in ("var_eps", "std", "rstd", "shift"))
        pad_src = sb("pad_src", [P, TILES], I32)
        pad_dst = sb("pad_dst", [P, TILES], I32)
        bound_i = sb("bound_i", [N_BND, 1], I32)
        bound = sb("bound", [N_BND, 1])
        sample = sb("sample", [N_BND, N_SAMP], I32)
        below = sb("below", [N_BND, SAMPLE])
        block_i = sb("block_i", [N_BND, 1], I32)
        block = sb("block", [N_BND, 1])
        count = sb("count", [N_BND, 2])
        within = sb("within", [N_BND, SAMPLE], I32)
        first = sb("first", [N_BND, 1])
        unsorted = sb("unsorted", [SORT_P, 1])
        first_row = sb("first_row", [1, N_BND])
        run_len = sb("run_len", [1, N_WIN])
        flags = sb("flags", [1, 8])
        first_i = sb("first_i", [1, N_BND], I32)
        general_i = sb("general_i", [1, 1], I32)
        ids_i = sb("ids_i", [P, NODES_W], I32)
        flat = rows[:, :, :].rearrange("p a b -> p (a b)")
        dst_here = flat[0:SORT_P, 0:SORT_F].bitcast(I32)
        dst_next = flat[0:SORT_P, SORT_F:2 * SORT_F].bitcast(I32)
        falls = flat[0:SORT_P, 2 * SORT_F:3 * SORT_F]
        gen_src = sb("gen_src", [GEN_E, 1], I32)
        gen_dst = sb("gen_dst", [GEN_E, 1], I32)
        gen_row = sb("gen_row", [GEN_E, GEN_E], I32)
        gen_dst_f = sb("gen_dst_f", [GEN_E, 1])
        gen_same = sb("gen_same", [GEN_E, GEN_E])
        gen_before = sb("gen_before", [GEN_E, GEN_E])
        earlier = sb("earlier", [GEN_E, GEN_E])
        gen_dup = sb("gen_dup", [GEN_E, 1])
        gen_to = sb("gen_to", [GEN_E, 1])
        gen_to_i = sb("gen_to_i", [GEN_E, 1], I32)
        gen_in = sb("gen_in", [GEN_E, F_HID])
        gen_sum = sb("gen_sum", [GEN_E, F_HID])

        def banks(name):
            return ctx.enter_context(nc.psum_tensor(name, [P, 2, 512], F32))
        sum_ps, t_ps, a_ps, b_ps = banks("sum_ps"), banks("t_ps"), banks("a_ps"), banks("b_ps")

        setup_dma = sem("setup_dma")
        pad_dma = sem("pad_dma")
        sample_dma = sem("sample_dma")
        sample_in = sem("sample_in")
        weights_in = sem("weights_in")
        eps_in = sem("eps_in")
        pads_set = sem("pads_set")
        tail_set = sem("tail_set")
        consts_set = sem("consts_set")
        block_ready = sem("block_ready")
        within_in = sem("within_in")
        first_ready = sem("first_ready")
        first_across = sem("first_across")
        keep_ready = sem("keep_ready")
        keep_across = sem("keep_across")
        general_ready = sem("general_ready")
        src_loaded = [sem(f"src_loaded{j}") for j in range(WINS)]
        dst_loaded = [sem(f"dst_loaded{j}") for j in range(WINS)]
        own_loaded = sem("own_loaded")
        resid_loaded = sem("resid_loaded")
        rows_landed = [sem(f"rows_landed{t}") for t in range(RING)]
        onehot_built = sem("onehot_built")
        groups_summed = sem("groups_summed")
        z_done = sem("z_done")
        t_ready = sem("t_ready")
        zt_done = sem("zt_done")
        a_ready = sem("a_ready")
        at_done = sem("at_done")
        b_ready = sem("b_ready")
        b_read = sem("b_read")
        staged_done = sem("staged_done")
        var_ready = sem("var_ready")
        std_ready = sem("std_ready")
        rstd_ready = sem("rstd_ready")
        shift_ready = sem("shift_ready")
        stored = sem("stored")
        dve_step = sem("dve_step")
        gen_in_dma = sem("gen_in_dma")
        gen_scaled = sem("gen_scaled")
        gen_base_dma = sem("gen_base_dma")
        gen_gathered = sem("gen_gathered")
        gen_matrix = sem("gen_matrix")
        gen_summed = sem("gen_summed")
        gen_new = sem("gen_new")
        gen_scattered = sem("gen_scattered")
        gen_mask = sem("gen_mask")
        gen_chain = sem("gen_chain")
        ids_moved = sem("ids_moved")
        ids_wrapped = sem("ids_wrapped")
        ln_chain = sem("ln_chain")

        CREDIT = 2 * NG

        def groups_after(w):
            return w * NG + NG + CREDIT

        def load_flag(eng):
            eng.wait_ge(general_ready, 1)
            return eng.value_load(general_i[0:1, 0:1], min_val=0, max_val=1)

        block_ctx = ctx.enter_context(nc.Block())

        @block_ctx.sync
        def _(sp):
            sp.dma_start(dst_here, dst.rearrange("(p f) -> p f", p=SORT_P)).then_inc(setup_dma, 16)
            sp.wait_ge(tail_set, 1)
            sp.dma_start(dst_next[0:SORT_P - 1, :],
                         dst[1:1 + (SORT_P - 1) * SORT_F].rearrange("(p f) -> p f", f=SORT_F)).then_inc(setup_dma, 16)
            sp.dma_start(dst_next[SORT_P - 1:SORT_P, 0:SORT_F - 1],
                         dst[1 + (SORT_P - 1) * SORT_F:N_EDGES].rearrange("(p f) -> p f", p=1)).then_inc(setup_dma, 16)
            with nc.allow_non_contiguous_dma(reason="one sample of each block"):
                sp.dma_start(samples_dram.rearrange("(a b) -> a b", b=1),
                             dst.rearrange("(a b) -> a b", b=SAMPLE)[:, 0:1]).then_inc(sample_dma, 16)
            sp.wait_ge(sample_dma, 16)
            sp.dma_start(sample[:, :], samples_dram.partition_broadcast(N_BND)).then_inc(sample_in, 16)
            for pad, full in ((src_pad, src), (dst_pad, dst)):
                sp.dma_start(pad[0:N_EDGES].rearrange("(a b) -> a b", a=160),
                             full.rearrange("(a b) -> a b", a=160)).then_inc(pad_dma, 16)
            sp.wait_ge(pads_set, 2)
            for pad, tile in ((src_pad, pad_src), (dst_pad, pad_dst)):
                sp.dma_start(pad[N_EDGES:].rearrange("(p t) -> p t", t=TILES), tile[:, :]).then_inc(pad_dma, 16)
            general = load_flag(sp)
            sp.wait_ge(pad_dma, 64)

            def load_window(w, j, r):
                first_edge = sp.value_load(first_i[0:1, bass.ds(w, 1)], min_val=0, max_val=N_EDGES)
                sp.dma_start(src_idx[:, j, :], src_pad[bass.ds(first_edge, ROOM)].rearrange("(p t) -> p t", t=TILES)
                             ).then_inc(src_loaded[j], 16)
                sp.dma_start(dst_idx[:, j, :], dst_pad[bass.ds(first_edge, ROOM)].rearrange("(p t) -> p t", t=TILES)
                             ).then_inc(dst_loaded[j], 16)

            def by_window(rows_ap):
                return rows_ap.rearrange("(j p) f -> p j f", p=NODES_W)

            def round_loads(r, layer, first_round):
                for j in range(WINS):
                    if not (layer == 0 and first_round):
                        sp.wait_ge(groups_summed, groups_after((r - 1) * WINS + j))
                        sp.nop(nofuse=True)
                    load_window(r * WINS + j - layer * N_WIN, j, r)

            def own_load(r, layer):
                node = r * NODES_R - layer * N_NODES
                F = F_TAB[layer]
                with sp.If(general):
                    sp.dma_start(own[:, :, 0:F], by_window(base_table[layer][bass.ds(node, NODES_R), :])
                                 ).then_inc(own_loaded, 16)
                with sp.Else():
                    sp.dma_start(own[:, :, 0:F], by_window(table[layer][bass.ds(node, NODES_R), :])
                                 ).then_inc(own_loaded, 16)

            for layer in range(2):
                F = F_TAB[layer]
                r0 = layer * ROUNDS
                round_loads(r0, layer, True)
                if layer:
                    sp.wait_ge(stored, 16 * ROUNDS)
                    sp.wait_ge(z_done, r0 * WINS)
                    sp.nop(nofuse=True)
                with sp.If(general):
                    base0 = 16 * layer * ROUNDS
                    with sp.Fori(0, ROUNDS) as s:
                        in0 = layer * (16 * ROUNDS + 48 * GEN_TILES)
                        sp.dma_start(own[:, :, 0:F], by_window(table[layer][bass.ds(s * NODES_R, NODES_R), :])
                                     ).then_inc(gen_in_dma, 16)
                        sp.wait_ge(gen_scaled, layer * ROUNDS + s + 1)
                        sp.nop(nofuse=True)
                        sp.dma_start(by_window(base_table[layer][bass.ds(s * NODES_R, NODES_R), :]), z[:, :, 0:F]
                                     ).then_inc(gen_base_dma, 16)
                        sp.wait_ge(gen_base_dma, base0 + s * 16 + 16)
                        sp.nop(nofuse=True)
                    with sp.Fori(0, GEN_TILES) as i:
                        at = i * GEN_E
                        sp.dma_start(gen_src[:, :], src[bass.ds(at, GEN_E)].rearrange("(p o) -> p o", o=1)
                                     ).then_inc(gen_in_dma, 16)
                        sp.dma_start(gen_dst[:, :], dst[bass.ds(at, GEN_E)].rearrange("(p o) -> p o", o=1)
                                     ).then_inc(gen_in_dma, 16)
                        sp.dma_start(gen_row[:, :], dst[bass.ds(at, GEN_E)].partition_broadcast(GEN_E)
                                     ).then_inc(gen_in_dma, 16)
                        sp.wait_ge(gen_scattered, layer * 16 * GEN_TILES + i * 16 + 16)
                        sp.nop(nofuse=True)
                with sp.Else():
                    sp.nop()
                own_load(r0, layer)
                with sp.Fori(r0 + 1, r0 + ROUNDS) as r:
                    round_loads(r, layer, False)
                    sp.wait_ge(z_done, r * WINS)
                    sp.nop(nofuse=True)
                    own_load(r, layer)
                    if layer:
                        sp.wait_ge(z_done, r * WINS + 1)
                        sp.nop(nofuse=True)
                        sp.dma_start(resid[:, :, :],
                                     by_window(x[bass.ds(r * NODES_R - N_NODES - NODES_R, NODES_R), :])
                                     ).then_inc(resid_loaded, 16)
            sp.wait_ge(groups_summed, groups_after(2 * N_WIN - WINS))
            sp.dma_start(dst_idx[:, 0, :], dst_pad[N_EDGES:].rearrange("(p t) -> p t", t=TILES)
                         ).then_inc(dst_loaded[0], 16)
            sp.wait_ge(shift_ready, ROUNDS - 1)
            sp.dma_start(resid[:, :, :], by_window(x[N_NODES - NODES_R:N_NODES, :])).then_inc(resid_loaded, 16)

        @block_ctx.gpsimd
        def _(pool):
            pool.memset(dst_next, PAD_NODE).then_inc(tail_set, 1)
            pool.memset(pad_src[:, :], 0).then_inc(pads_set, 1)
            pool.memset(pad_dst[:, :], PAD_NODE).then_inc(pads_set, 1)
            pool.memset(ones[:, :], 1.0).then_inc(consts_set, 1)
            pool.iota(bound_i[:, :], pattern=[[0, 1]], base=0, channel_multiplier=NODES_W).then_inc(consts_set, 1)
            pool.iota(ids_i[:, :], pattern=[[1, NODES_W]], base=0, channel_multiplier=0).then_inc(consts_set, 1)
            pool.wait_ge(consts_set, 3)
            pool.affine_select(out=ident[:, :], in_=ones[:, :], compare_op=ALU.is_equal, fill=0.0, base=0,
                               pattern=[[-1, P]], channel_multiplier=1).then_inc(consts_set, 1)
            pool.affine_select(out=earlier[:, :], in_=ones[0:GEN_E, 0:GEN_E], compare_op=ALU.is_gt, fill=0.0,
                               base=0, pattern=[[-1, GEN_E]], channel_multiplier=1).then_inc(gen_mask, 1)
            pool.wait_ge(block_ready, 1)
            pool.indirect_dma_start(out=within[:, :], out_offset=None, in_=dst.rearrange("(a b) -> a b", b=SAMPLE),
                                    in_offset=bass.IndirectOffsetOnAxis(ap=block_i[:, 0:1], axis=0)
                                    ).then_inc(within_in, 16)
            general = load_flag(pool)

            for layer in range(2):
                F = F_TAB[layer]
                if layer:
                    pool.wait_ge(stored, 16 * ROUNDS)
                with pool.If(general):
                    per_layer = 16 * ROUNDS + 48 * GEN_TILES
                    with pool.Fori(0, GEN_TILES) as i:
                        pool.wait_ge(gen_in_dma, layer * per_layer + 16 * ROUNDS + i * 48 + 48)
                        pool.nop(nofuse=True)
                        for tile, tab, idx in ((gen_in, table[layer], gen_src), (gen_sum, base_table[layer], gen_dst)):
                            pool.indirect_dma_start(out=tile[:, 0:F], out_offset=None, in_=tab,
                                                    in_offset=bass.IndirectOffsetOnAxis(ap=idx[:, 0:1], axis=0)
                                                    ).then_inc(gen_gathered, 16)
                        pool.wait_ge(gen_new, layer * GEN_TILES + i + 1)
                        pool.nop(nofuse=True)
                        pool.indirect_dma_start(out=base_table[layer],
                                                out_offset=bass.IndirectOffsetOnAxis(ap=gen_to_i[:, 0:1], axis=0),
                                                in_=gen_sum[:, 0:F], in_offset=None,
                                                bounds_check=N_NODES - 1, oob_is_err=False
                                                ).then_inc(gen_scattered, 16)
                        pool.wait_ge(gen_scattered, layer * 16 * GEN_TILES + i * 16 + 16)
                with pool.Else():
                    pool.nop()

                def gather_window(w, j, r):
                    pool.wait_ge(src_loaded[j], 16 * r + 16)
                    for g, (t0, t1) in enumerate(GROUPS):
                        pool.wait_ge(groups_summed, w * NG + g + 1)
                        pool.nop(nofuse=True)
                        for t in range(t0, t1):
                            slot = (j % 2) * TILES + t
                            pool.indirect_dma_start(out=rows[:, slot, 0:F], out_offset=None, in_=table[layer],
                                                    in_offset=bass.IndirectOffsetOnAxis(ap=src_idx[:, j, t:t + 1], axis=0)
                                                    ).then_inc(rows_landed[slot], 16)

                with pool.Fori(layer * ROUNDS, layer * ROUNDS + ROUNDS) as r:
                    for j in range(WINS):
                        gather_window(r * WINS + j, j, r)

        @block_ctx.tensor
        def _(pe):
            pe.wait_ge(consts_set, 4)
            pe.wait_ge(first_ready, 2)
            nc.tensor.matmul(a_ps[0:1, 0, 0:N_BND], first[:, :], ident[0:N_BND, 0:N_BND], start=True, stop=True)
            nc.tensor.matmul(a_ps[0:1, 1, 0:1], unsorted[:, :], ones[0:SORT_P, 0:1], start=True, stop=True
                             ).then_inc(first_across, 1)
            pe.wait_ge(keep_ready, 1)
            nc.tensor.matmul(b_ps[0:NODES_W, 0, 0:1], ones[0:1, 0:NODES_W], flags[0:1, 4:5], start=True, stop=True
                             ).then_inc(keep_across, 1)
            general = load_flag(pe)
            pe.wait_ge(weights_in, 16 * 8)
            pe.sem_inc(groups_summed, CREDIT)

            for layer in range(2):
                F, K = F_TAB[layer], KA[layer]
                r0 = layer * ROUNDS
                with pe.If(general):
                    with pe.Fori(0, GEN_TILES) as i:
                        pe.wait_ge(gen_matrix, layer * GEN_TILES + i + 1)
                        pe.wait_ge(gen_gathered, layer * 32 * GEN_TILES + i * 32 + 32)
                        nc.tensor.matmul(b_ps[0:GEN_E, 0, 0:F], gen_same[:, :], gen_in[:, 0:F], start=True, stop=True
                                         ).then_inc(gen_summed, 1)
                with pe.Else():
                    pe.nop()

                def sum_window(w, j, r, bank_waits=True):
                    pe.wait_ge(onehot_built, w + 1)
                    if bank_waits:
                        pe.wait_ge(z_done, w - 1)
                    for t0, t1 in GROUPS:
                        for t in range(t0, t1):
                            slot = (j % 2) * TILES + t
                            pe.wait_ge(rows_landed[slot], 16 * (2 * r + j // 2 + 1))
                            mm = nc.tensor.matmul(sum_ps[0:NODES_W, j % 2, 0:F], onehot[:, j % 2, t, :],
                                                  rows[:, slot, 0:F], start=(t == 0), stop=(t == TILES - 1))
                        mm.then_inc(groups_summed, 1)

                def transpose_round(q):
                    for j in range(WINS):
                        pe.wait_ge(z_done, q * WINS + j + 1)
                        if j >= 2:
                            pe.wait_ge(zt_done, q * WINS + j - 1)
                        for k in range(K):
                            mm = nc.tensor.transpose(t_ps[:, j % 2, k * NODES_W:(k + 1) * NODES_W],
                                                     z[:, j, k * P:(k + 1) * P], ident[0:NODES_W, 0:NODES_W])
                        mm.then_inc(t_ready, 1)

                def first_product(q):
                    pe.wait_ge(zt_done, q * WINS + WINS)
                    for m in range(MB):
                        if m >= 2:
                            pe.wait_ge(at_done, q * MB + m - 1)
                        for k in range(K):
                            mm = nc.tensor.matmul(a_ps[:, m % 2, 0:NODES_R], wa[layer][:, k, m * P:(m + 1) * P],
                                                  zT[:, k, :], start=(k == 0), stop=(k == K - 1))
                        mm.then_inc(a_ready, 1)

                def second_product(q, windows):
                    pe.wait_ge(at_done, q * MB + MB)
                    for j in windows:
                        if j >= 2:
                            pe.wait_ge(b_read, q * WINS + j - 1)
                        for k in range(MB):
                            mm = nc.tensor.matmul(b_ps[0:NODES_W, j % 2, 0:F_RES[layer]],
                                                  aT[:, k, j * NODES_W:(j + 1) * NODES_W], wb[layer][:, k, :],
                                                  start=(k == 0), stop=(k == MB - 1))
                        mm.then_inc(b_ready, 1)

                for j in range(WINS):
                    sum_window(r0 * WINS + j, j, r0, bank_waits=(layer == 1 or j >= 2))
                with pe.Fori(r0 + 1, r0 + ROUNDS) as r:
                    sum_window(r * WINS, 0, r)
                    transpose_round(r - 1)
                    sum_window(r * WINS + 1, 1, r)
                    first_product(r - 1)
                    sum_window(r * WINS + 2, 2, r)
                    second_product(r - 1, (0, 1))
                    sum_window(r * WINS + 3, 3, r)
                    second_product(r - 1, (2, 3))
                q = r0 + ROUNDS - 1
                transpose_round(q)
                first_product(q)
                pe.wait_ge(b_read, q * WINS)
                second_product(q, range(WINS))

        @block_ctx.scalar
        def _(act):
            with nc.allow_non_contiguous_dma(reason="biases to partitions, once"):
                for layer, (a, b) in enumerate(((w1a, w1b), (w2a, w2b))):
                    act.dma_start(wa[layer][:, :, :], a.rearrange("(k p) n -> p k n", p=P)).then_inc(weights_in, 16)
                    act.dma_start(wb[layer][:, :, :], b.rearrange("(k p) n -> p k n", p=P)).then_inc(weights_in, 16)
                for layer, (a, b) in enumerate(((b1a, b1b), (b2a, b2b))):
                    act.dma_start(ba[layer][:, :], a.rearrange("(m p) -> p m", p=P)).then_inc(weights_in, 16)
                    act.dma_start(bb[layer][:, :], b.partition_broadcast(NODES_W)).then_inc(weights_in, 16)
                for layer, e in enumerate((eps1, eps2)):
                    act.dma_start(eps[:, layer:layer + 1], e.partition_broadcast(NODES_W)).then_inc(eps_in, 16)
            act.wait_ge(weights_in, 16 * 8)

            for layer in range(2):
                K = KA[layer]
                r0 = layer * ROUNDS

                def dense_out(q):
                    for j in range(WINS):
                        act.wait_ge(t_ready, q * WINS + j + 1)
                        nc.scalar.activation(
                            zT[:, 0:K, j * NODES_W:(j + 1) * NODES_W],
                            t_ps[:, j % 2, 0:K * NODES_W].rearrange("p (k n) -> p k n", k=K),
                            ACT.Copy).then_inc(zt_done, 1)
                    for m in range(MB):
                        act.wait_ge(a_ready, q * MB + m + 1)
                        nc.scalar.activation(aT[:, m, :], a_ps[:, m % 2, 0:NODES_R], ACT.Relu,
                                             bias=ba[layer][:, m:m + 1]).then_inc(at_done, 1)
                    if layer == 0:
                        for j in range(WINS):
                            act.wait_ge(b_read, q * WINS + j + 1)
                            nc.scalar.activation(staged[:, j, :], staged[:, j, :], ACT.Relu).then_inc(staged_done, 1)
                    else:
                        act.wait_ge(var_ready, q - ROUNDS + 1)
                        nc.scalar.activation(std[:, :], var_eps[:, :], ACT.Sqrt).then_inc(std_ready, 1)
                        act.wait_ge(shift_ready, q - ROUNDS + 1)
                        for j in range(WINS):
                            nc.scalar.activation(staged[:, j, 0:F_OUT], staged[:, j, 0:F_OUT], ACT.Identity,
                                                 scale=rstd[:, j:j + 1], bias=shift[:, j:j + 1]
                                                 ).then_inc(staged_done, 1)
                    act.wait_ge(staged_done, q * WINS + WINS)
                    node = q * NODES_R - layer * N_NODES
                    act.dma_start(result[layer][bass.ds(node, NODES_R), :].rearrange("(j p) f -> p j f", p=NODES_W),
                                  staged[:, :, 0:F_RES[layer]]).then_inc(stored, 16)
                    act.wait_ge(stored, q * 16 + 16)

                with act.Fori(r0, r0 + ROUNDS - 1) as q:
                    dense_out(q)
                dense_out(r0 + ROUNDS - 1)

        @block_ctx.vector
        def _(dve):
            steps = [0]

            def link(ins):
                steps[0] += 1
                ins.then_inc(dve_step, 1)
                dve.wait_ge(dve_step, steps[0])

            dve.wait_ge(consts_set, 3)
            link(nc.vector.tensor_copy(bound[:, :], bound_i[:, :]))
            nc.vector.tensor_copy(node_ids[:, :], ids_i[:, :])
            dve.wait_ge(sample_in, 16)
            link(nc.vector.tensor_scalar(below[:, 0:N_SAMP], sample[:, :], bound[:, 0:1], None, ALU.is_lt))
            link(nc.vector.tensor_reduce(out=count[:, 0:1], in_=below[:, 0:N_SAMP], axis=AX_X, op=ALU.add))
            link(nc.vector.tensor_scalar(block[:, :], count[:, 0:1], 1.0, 0.0, ALU.subtract, ALU.max))
            nc.vector.tensor_copy(block_i[:, :], block[:, :]).then_inc(block_ready, 1)
            dve.wait_ge(setup_dma, 48)
            link(nc.vector.tensor_tensor(falls, dst_here, dst_next, ALU.is_gt))
            nc.vector.tensor_reduce(out=unsorted[:, :], in_=falls, axis=AX_X, op=ALU.add).then_inc(first_ready, 1)
            dve.wait_ge(within_in, 16)
            link(nc.vector.tensor_scalar(below[:, :], within[:, :], bound[:, 0:1], None, ALU.is_lt))
            link(nc.vector.tensor_reduce(out=count[:, 1:2], in_=below[:, :], axis=AX_X, op=ALU.add))
            nc.vector.scalar_tensor_tensor(out=first[:, :], in0=block[:, :], scalar=float(SAMPLE), in1=count[:, 1:2],
                                           op0=ALU.mult, op1=ALU.add).then_inc(first_ready, 1)
            dve.wait_ge(first_across, 1)
            link(nc.vector.tensor_copy(first_row[:, :], a_ps[0:1, 0, 0:N_BND]))
            link(nc.vector.tensor_tensor(run_len[:, :], first_row[:, 1:N_BND], first_row[:, 0:N_WIN], ALU.subtract))
            link(nc.vector.tensor_reduce(out=flags[:, 0:1], in_=run_len[:, :], axis=AX_X, op=ALU.max))
            link(nc.vector.tensor_scalar(flags[:, 1:2], flags[:, 0:1], float(ROOM), None, ALU.is_gt))
            link(nc.vector.tensor_scalar(flags[:, 2:3], a_ps[0:1, 1, 0:1], 0.0, None, ALU.is_gt))
            link(nc.vector.tensor_tensor(flags[:, 3:4], flags[:, 1:2], flags[:, 2:3], ALU.max))
            link(nc.vector.tensor_scalar(flags[:, 4:5], flags[:, 3:4], -1.0, 1.0, ALU.mult, ALU.add))
            nc.vector.tensor_scalar(flags[:, 5:6], flags[:, 3:4], float(N_EDGES), None, ALU.mult).then_inc(keep_ready, 1)
            dve.wait_ge(keep_ready, 1)
            link(nc.vector.tensor_scalar(first_row[:, :], first_row[:, :], flags[:, 4:5], flags[:, 5:6],
                                         ALU.mult, ALU.add))
            link(nc.vector.tensor_copy(first_i[:, :], first_row[:, :]))
            nc.vector.tensor_copy(general_i[:, :], flags[:, 3:4]).then_inc(general_ready, 1)
            dve.wait_ge(eps_in, 32)
            dve.wait_ge(keep_across, 1)
            nc.vector.tensor_scalar(gen_scale[:, :], eps[:, :], 1.0, None, ALU.add)
            link(nc.vector.tensor_scalar(own_scale[:, :], eps[:, :], b_ps[0:NODES_W, 0, 0:1], 1.0, ALU.mult, ALU.add))
            general = load_flag(dve)
            dve.wait_ge(weights_in, 16 * 8)
            dve.wait_ge(gen_mask, 1)

            def build_onehot(w, slot, dst_slot, r):
                dve.wait_ge(dst_loaded[dst_slot], 16 * r + 16)
                nc.vector.tensor_tensor(
                    onehot[:, slot, :, :], dst_idx[:, dst_slot, :].unsqueeze(2).broadcast_to([P, TILES, NODES_W]),
                    node_ids[:, :].unsqueeze(1).broadcast_to([P, TILES, NODES_W]), ALU.is_equal
                    ).then_inc(onehot_built, 1)
                dve.wait_ge(onehot_built, w + 1)
                nc.vector.tensor_scalar(node_ids[:, :], node_ids[:, :], float(NODES_W), None, ALU.add
                                        ).then_inc(ids_moved, 1)
                dve.wait_ge(ids_moved, w + 1)
                if dst_slot == WINS - 1:
                    nc.vector.tensor_scalar(ids_over[:, :], node_ids[:, :], float(N_NODES), -float(N_NODES),
                                            ALU.is_ge, ALU.mult).then_inc(ids_wrapped, 1)
                    dve.wait_ge(ids_wrapped, 2 * r + 1)
                    nc.vector.tensor_tensor(node_ids[:, :], node_ids[:, :], ids_over[:, :], ALU.add
                                            ).then_inc(ids_wrapped, 1)
                    dve.wait_ge(ids_wrapped, 2 * r + 2)

            build_onehot(0, 0, 0, 0)

            for layer in range(2):
                F, FR = F_TAB[layer], F_RES[layer]
                r0 = layer * ROUNDS
                with dve.If(general):
                    with dve.Fori(0, ROUNDS) as s:
                        per_layer = 16 * ROUNDS + 48 * GEN_TILES
                        dve.wait_ge(gen_in_dma, layer * per_layer + s * 16 + 16)
                        nc.vector.tensor_scalar(z[:, :, 0:F], own[:, :, 0:F], gen_scale[:, layer:layer + 1], None,
                                                ALU.mult).then_inc(gen_scaled, 1)
                    with dve.Fori(0, GEN_TILES) as i:
                        n = i + layer * GEN_TILES
                        dve.wait_ge(gen_in_dma, layer * per_layer + 16 * ROUNDS + i * 48 + 48)
                        nc.vector.tensor_copy(gen_dst_f[:, :], gen_dst[:, :]).then_inc(gen_chain, 1)
                        dve.wait_ge(gen_chain, 5 * n + 1)
                        nc.vector.tensor_scalar(gen_same[:, :], gen_row[:, :], gen_dst_f[:, 0:1], None,
                                                ALU.is_equal).then_inc(gen_matrix, 1)
                        dve.wait_ge(gen_matrix, n + 1)
                        nc.vector.tensor_tensor(gen_before[:, :], gen_same[:, :], earlier[:, :], ALU.mult
                                                ).then_inc(gen_chain, 1)
                        dve.wait_ge(gen_chain, 5 * n + 2)
                        nc.vector.tensor_reduce(out=gen_dup[:, :], in_=gen_before[:, :], axis=AX_X, op=ALU.add
                                                ).then_inc(gen_chain, 1)
                        dve.wait_ge(gen_chain, 5 * n + 3)
                        nc.vector.scalar_tensor_tensor(out=gen_to[:, :], in0=gen_dup[:, :], scalar=float(N_NODES),
                                                       in1=gen_dst_f[:, :], op0=ALU.mult, op1=ALU.add
                                                       ).then_inc(gen_chain, 1)
                        dve.wait_ge(gen_chain, 5 * n + 4)
                        nc.vector.tensor_copy(gen_to_i[:, :], gen_to[:, :]).then_inc(gen_chain, 1)
                        dve.wait_ge(gen_chain, 5 * n + 5)
                        dve.wait_ge(gen_gathered, 32 * n + 32)
                        dve.wait_ge(gen_summed, n + 1)
                        nc.vector.tensor_tensor(gen_sum[:, 0:F], gen_sum[:, 0:F], b_ps[0:GEN_E, 0, 0:F], ALU.add
                                                ).then_inc(gen_new, 1)
                with dve.Else():
                    dve.nop()

                def window_z(w, j, r, reused=True):
                    dve.wait_ge(groups_summed, groups_after(w))
                    dve.wait_ge(own_loaded, 16 * r + 16)
                    if reused:
                        dve.wait_ge(t_ready, (r - 1) * WINS + j + 1)
                    nc.vector.scalar_tensor_tensor(out=z[:, j, 0:F], in0=own[:, j, 0:F],
                                                   scalar=own_scale[:, layer:layer + 1],
                                                   in1=sum_ps[0:NODES_W, j % 2, 0:F],
                                                   op0=ALU.mult, op1=ALU.add).then_inc(z_done, 1)

                def result_window(q, j):
                    v = q * WINS + j
                    dve.wait_ge(b_ready, v + 1)
                    if layer == 0:
                        nc.vector.tensor_tensor(staged[:, j, :], b_ps[0:NODES_W, j % 2, 0:FR], bb[0][:, :], ALU.add
                                                ).then_inc(b_read, 1)
                        return
                    y = staged[:, j, 0:FR]
                    n = v - N_WIN
                    nc.vector.tensor_tensor(y, b_ps[0:NODES_W, j % 2, 0:FR], bb[1][:, :], ALU.add).then_inc(b_read, 1)
                    dve.wait_ge(b_read, v + 1)
                    dve.wait_ge(resid_loaded, (q - ROUNDS) * 16 + 16)
                    nc.vector.tensor_tensor(y, y, resid[:, j, :], ALU.add).then_inc(ln_chain, 1)
                    dve.wait_ge(ln_chain, 3 * n + 1)
                    nc.vector.bn_stats(out=stats[:, :], in_=y).then_inc(ln_chain, 1)
                    dve.wait_ge(ln_chain, 3 * n + 2)
                    dve.nop(nofuse=True)
                    nc.vector.bn_aggr(out=meanvar[:, j, :], in_=stats[:, :]).then_inc(ln_chain, 1)
                    dve.wait_ge(ln_chain, 3 * n + 3)

                def norm_factors(q):
                    if layer == 0:
                        return
                    n = q - ROUNDS
                    nc.vector.tensor_scalar(var_eps[:, :], meanvar[:, :, 1], LN_EPS, None, ALU.add
                                            ).then_inc(var_ready, 1)
                    dve.wait_ge(std_ready, n + 1)
                    nc.vector.reciprocal(rstd[:, :], std[:, :]).then_inc(rstd_ready, 1)
                    dve.wait_ge(rstd_ready, n + 1)
                    nc.vector.scalar_tensor_tensor(out=shift[:, :], in0=meanvar[:, :, 0], scalar=-1.0, in1=rstd[:, :],
                                                   op0=ALU.mult, op1=ALU.mult).then_inc(shift_ready, 1)

                def sums(r, j, reused=True):
                    w = r * WINS + j
                    if reused or j:
                        dve.wait_ge(groups_summed, groups_after(w - 1))
                    build_onehot(w + 1, (j + 1) % 2, (j + 1) % WINS, r + (j + 1) // WINS)
                    window_z(w, j, r, reused)

                for j in range(WINS):
                    sums(r0, j, reused=layer == 1)
                with dve.Fori(r0 + 1, r0 + ROUNDS) as r:
                    sums(r, 0)
                    sums(r, 1)
                    sums(r, 2)
                    result_window(r - 1, 0)
                    result_window(r - 1, 1)
                    sums(r, 3)
                    result_window(r - 1, 2)
                    result_window(r - 1, 3)
                    norm_factors(r - 1)
                for j in range(WINS):
                    result_window(r0 + ROUNDS - 1, j)
                norm_factors(r0 + ROUNDS - 1)


_INS = ['x', 'src', 'dst', 'L0_gnn_W1a', 'L0_gnn_b1a', 'L0_gnn_W1b', 'L0_gnn_b1b', 'L0_gnn_W2a', 'L0_gnn_b2a',
        'L0_gnn_W2b', 'L0_gnn_b2b', 'L0_gnn_eps1', 'L0_gnn_eps2']


def kernel(**inputs):
    import numpy as _np
    import concourse.bacc as _bacc
    from concourse import mybir as _mybir
    from concourse.bass_utils import run_bass_kernel_spmd as _run

    nc = _bacc.Bacc("TRN2", target_bir_lowering=False, num_devices=1)
    arrays, args = {}, []
    for name in _INS:
        a = _np.ascontiguousarray(inputs[name])
        if a.ndim == 0:
            a = a.reshape(1)
        arrays[f"in_{name}"] = a
        args.append(nc.dram_tensor(f"in_{name}", a.shape, _mybir.dt.from_np(a.dtype), kind="ExternalInput").ap())
    out = nc.dram_tensor("out", (N_NODES, F_OUT), _mybir.dt.float32, kind="ExternalOutput").ap()
    build(nc, *args, out)
    r = _run(nc, [arrays], core_ids=[0])
    return r.results[0]["out"]
```

```python
import concourse.bass as bass
from concourse import mybir
from contextlib import ExitStack

F32 = mybir.dt.float32
I32 = mybir.dt.int32
ALU = mybir.AluOpType
ACT = mybir.ActivationFunctionType
AX_X = mybir.AxisListType.X

N_NODES, N_EDGES = 12500, 200000
F_IN, F_HID, F_OUT = 256, 512, 256
P = 128
NODES_W = 125
WINS = 4
ROUNDS = N_NODES // (NODES_W * WINS)
N_WIN = ROUNDS * WINS
NODES_R = NODES_W * WINS
TILES = 17
ROOM = TILES * P
GROUPS = [(0, 4), (4, 8), (8, 12), (12, TILES)]
NG = len(GROUPS)
RING = 2 * TILES
PAD_NODE = 1 << 23
SAMPLE = 500
N_SAMP = N_EDGES // SAMPLE
N_BND = N_WIN + 1
SORT_P = 125
SORT_F = N_EDGES // SORT_P
GEN_E = 125
GEN_TILES = N_EDGES // GEN_E
KB = [F_IN // P, F_HID // P]
MB = F_HID // P
F_TAB = [F_IN, F_HID]
F_RES = [F_HID, F_OUT]
LN_EPS = 1e-5


def build(nc, x, src, dst, w1a, b1a, w1b, b1b, w2a, b2a, w2b, b2b, eps1, eps2, out):
    ctx = ExitStack()
    with ctx:
        def sb(name, shape, dt=F32):
            return ctx.enter_context(nc.sbuf_tensor(name, shape, dt))

        def sem(name):
            return ctx.enter_context(nc.semaphore(name))

        def scratch(name, shape, dt=F32):
            return nc.dram_tensor(name, shape, dt, kind="Internal").ap()

        hidden = scratch("hidden", [N_NODES, F_HID])
        src_pad = scratch("src_pad", [N_EDGES + ROOM], I32)
        dst_pad = scratch("dst_pad", [N_EDGES + ROOM], I32)
        samples_dram = scratch("samples_dram", [N_SAMP], I32)
        base_table = [scratch("base_table1", [N_NODES, F_IN]), scratch("base_table2", [N_NODES, F_HID])]
        table = [x, hidden]
        result = [hidden, out]

        rows = sb("rows", [P, RING, F_HID])
        onehot = sb("onehot", [P, 2, TILES, NODES_W])
        src_idx = sb("src_idx", [P, WINS, TILES], I32)
        dst_idx = sb("dst_idx", [P, WINS, TILES], I32)
        node_ids = sb("node_ids", [P, NODES_W])
        ids_over = sb("ids_over", [P, NODES_W])
        own = sb("own", [NODES_W, WINS, F_HID])
        z = sb("z", [NODES_W, WINS, F_HID])
        zT = sb("zT", [P, KB[0], NODES_R])
        aT = sb("aT", [P, MB, NODES_R])
        hT = sb("hT", [P, MB, NODES_R])
        staged = sb("staged", [NODES_W, WINS, F_HID])
        resid = sb("resid", [NODES_W, WINS, F_OUT])
        w1a_s = sb("w1a_s", [P, KB[0], F_HID])
        w1b_s, w2a_s = (sb(n, [P, MB, F_HID]) for n in ("w1b_s", "w2a_s"))
        w2b_s = sb("w2b_s", [P, MB, F_OUT])
        w_last = [w2a_s, w2b_s]
        b1a_s, b1b_s, b2a_s = (sb(n, [P, MB]) for n in ("b1a_s", "b1b_s", "b2a_s"))
        b2b_s = sb("b2b_s", [NODES_W, F_OUT])
        ident = sb("ident", [P, P])
        ones = sb("ones", [P, P])
        eps = sb("eps", [NODES_W, 2])
        own_scale = sb("own_scale", [NODES_W, 2])
        gen_scale = sb("gen_scale", [NODES_W, 2])
        stats = sb("stats", [NODES_W, 6])
        meanvar = sb("meanvar", [NODES_W, WINS, 2])
        var_eps, std, rstd, shift = (sb(n, [NODES_W, WINS]) for n in ("var_eps", "std", "rstd", "shift"))
        pad_src = sb("pad_src", [P, TILES], I32)
        pad_dst = sb("pad_dst", [P, TILES], I32)
        bound_i = sb("bound_i", [N_BND, 1], I32)
        bound = sb("bound", [N_BND, 1])
        sample = sb("sample", [N_BND, N_SAMP], I32)
        below = sb("below", [N_BND, SAMPLE])
        block_i = sb("block_i", [N_BND, 1], I32)
        block = sb("block", [N_BND, 1])
        count = sb("count", [N_BND, 2])
        within = sb("within", [N_BND, SAMPLE], I32)
        first = sb("first", [N_BND, 1])
        unsorted = sb("unsorted", [SORT_P, 1])
        first_row = sb("first_row", [1, N_BND])
        run_len = sb("run_len", [1, N_WIN])
        flags = sb("flags", [1, 8])
        first_i = sb("first_i", [1, N_BND], I32)
        general_i = sb("general_i", [1, 1], I32)
        ids_i = sb("ids_i", [P, NODES_W], I32)
        flat = rows[:, :, :].rearrange("p a b -> p (a b)")
        dst_here = flat[0:SORT_P, 0:SORT_F].bitcast(I32)
        dst_next = flat[0:SORT_P, SORT_F:2 * SORT_F].bitcast(I32)
        falls = flat[0:SORT_P, 2 * SORT_F:3 * SORT_F]
        gen_src = sb("gen_src", [GEN_E, 1], I32)
        gen_dst = sb("gen_dst", [GEN_E, 1], I32)
        gen_row = sb("gen_row", [GEN_E, GEN_E], I32)
        gen_dst_f = sb("gen_dst_f", [GEN_E, 1])
        gen_same = sb("gen_same", [GEN_E, GEN_E])
        gen_before = sb("gen_before", [GEN_E, GEN_E])
        earlier = sb("earlier", [GEN_E, GEN_E])
        gen_dup = sb("gen_dup", [GEN_E, 1])
        gen_to = sb("gen_to", [GEN_E, 1])
        gen_to_i = sb("gen_to_i", [GEN_E, 1], I32)
        gen_in = sb("gen_in", [GEN_E, F_HID])
        gen_sum = sb("gen_sum", [GEN_E, F_HID])

        def banks(name):
            return ctx.enter_context(nc.psum_tensor(name, [P, 2, 512], F32))
        sum_ps, t_ps, a_ps, b_ps = banks("sum_ps"), banks("t_ps"), banks("a_ps"), banks("b_ps")

        setup_dma = sem("setup_dma")
        pad_dma = sem("pad_dma")
        sample_dma = sem("sample_dma")
        sample_in = sem("sample_in")
        weights_in = sem("weights_in")
        eps_in = sem("eps_in")
        pads_set = sem("pads_set")
        tail_set = sem("tail_set")
        consts_set = sem("consts_set")
        block_ready = sem("block_ready")
        within_in = sem("within_in")
        first_ready = sem("first_ready")
        first_across = sem("first_across")
        keep_ready = sem("keep_ready")
        keep_across = sem("keep_across")
        general_ready = sem("general_ready")
        src_loaded = [sem(f"src_loaded{j}") for j in range(WINS)]
        dst_loaded = [sem(f"dst_loaded{j}") for j in range(WINS)]
        own_loaded = sem("own_loaded")
        resid_loaded = sem("resid_loaded")
        rows_landed = [sem(f"rows_landed{t}") for t in range(RING)]
        onehot_built = sem("onehot_built")
        groups_summed = sem("groups_summed")
        z_done = sem("z_done")
        t_ready = sem("t_ready")
        t_read = sem("t_read")
        a_ready = sem("a_ready")
        a_read = sem("a_read")
        b_ready = sem("b_ready")
        b_read = sem("b_read")
        staged_done = sem("staged_done")
        var_ready = sem("var_ready")
        std_ready = sem("std_ready")
        rstd_ready = sem("rstd_ready")
        shift_ready = sem("shift_ready")
        stored = sem("stored")
        dve_step = sem("dve_step")
        gen_own_in = sem("gen_own_in")
        gen_src_in = sem("gen_src_in")
        gen_dst_in = sem("gen_dst_in")
        gen_row_in = sem("gen_row_in")
        gen_scaled = sem("gen_scaled")
        gen_base_dma = sem("gen_base_dma")
        gen_rows_in = sem("gen_rows_in")
        gen_sum_in = sem("gen_sum_in")
        gen_matrix = sem("gen_matrix")
        gen_summed = sem("gen_summed")
        gen_new = sem("gen_new")
        gen_scattered = sem("gen_scattered")
        gen_mask = sem("gen_mask")
        gen_chain = sem("gen_chain")
        ids_moved = sem("ids_moved")
        ids_wrapped = sem("ids_wrapped")
        ln_chain = sem("ln_chain")

        CREDIT = 2 * NG

        def groups_after(w):
            return w * NG + NG + CREDIT

        def blocks_before(q, layer):
            return q * KB[layer] - layer * ROUNDS * (KB[1] - KB[0])

        def load_flag(eng):
            eng.wait_ge(general_ready, 1)
            return eng.value_load(general_i[0:1, 0:1], min_val=0, max_val=1)

        block_ctx = ctx.enter_context(nc.Block())

        @block_ctx.sync
        def _(sp):
            sp.dma_start(dst_here, dst.rearrange("(p f) -> p f", p=SORT_P)).then_inc(setup_dma, 16)
            sp.wait_ge(tail_set, 1)
            sp.dma_start(dst_next[0:SORT_P - 1, :],
                         dst[1:1 + (SORT_P - 1) * SORT_F].rearrange("(p f) -> p f", f=SORT_F)).then_inc(setup_dma, 16)
            sp.dma_start(dst_next[SORT_P - 1:SORT_P, 0:SORT_F - 1],
                         dst[1 + (SORT_P - 1) * SORT_F:N_EDGES].rearrange("(p f) -> p f", p=1)).then_inc(setup_dma, 16)
            with nc.allow_non_contiguous_dma(reason="one sample of each block"):
                sp.dma_start(samples_dram.rearrange("(a b) -> a b", b=1),
                             dst.rearrange("(a b) -> a b", b=SAMPLE)[:, 0:1]).then_inc(sample_dma, 16)
            sp.wait_ge(sample_dma, 16)
            sp.dma_start(sample[:, :], samples_dram.partition_broadcast(N_BND)).then_inc(sample_in, 16)
            for pad, full in ((src_pad, src), (dst_pad, dst)):
                sp.dma_start(pad[0:N_EDGES].rearrange("(a b) -> a b", a=160),
                             full.rearrange("(a b) -> a b", a=160)).then_inc(pad_dma, 16)
            sp.wait_ge(pads_set, 2)
            for pad, tile in ((src_pad, pad_src), (dst_pad, pad_dst)):
                sp.dma_start(pad[N_EDGES:].rearrange("(p t) -> p t", t=TILES), tile[:, :]).then_inc(pad_dma, 16)
            general = load_flag(sp)
            sp.wait_ge(pad_dma, 64)

            def load_window(w, j, r):
                first_edge = sp.value_load(first_i[0:1, bass.ds(w, 1)], min_val=0, max_val=N_EDGES)
                sp.dma_start(src_idx[:, j, :], src_pad[bass.ds(first_edge, ROOM)].rearrange("(p t) -> p t", t=TILES)
                             ).then_inc(src_loaded[j], 16)
                sp.dma_start(dst_idx[:, j, :], dst_pad[bass.ds(first_edge, ROOM)].rearrange("(p t) -> p t", t=TILES)
                             ).then_inc(dst_loaded[j], 16)

            def by_window(rows_ap):
                return rows_ap.rearrange("(j p) f -> p j f", p=NODES_W)

            def round_loads(r, layer, first_round):
                for j in range(WINS):
                    if not (layer == 0 and first_round):
                        sp.wait_ge(groups_summed, groups_after((r - 1) * WINS + j))
                        sp.nop(nofuse=True)
                    load_window(r * WINS + j - layer * N_WIN, j, r)

            def own_load(r, layer):
                node = r * NODES_R - layer * N_NODES
                F = F_TAB[layer]
                with sp.If(general):
                    sp.dma_start(own[:, :, 0:F], by_window(base_table[layer][bass.ds(node, NODES_R), :])
                                 ).then_inc(own_loaded, 16)
                with sp.Else():
                    sp.dma_start(own[:, :, 0:F], by_window(table[layer][bass.ds(node, NODES_R), :])
                                 ).then_inc(own_loaded, 16)

            for layer in range(2):
                F = F_TAB[layer]
                r0 = layer * ROUNDS
                round_loads(r0, layer, True)
                if layer:
                    sp.wait_ge(stored, 16 * ROUNDS)
                    sp.wait_ge(z_done, r0 * WINS)
                    sp.nop(nofuse=True)
                with sp.If(general):
                    base0 = 16 * layer * ROUNDS
                    with sp.Fori(0, ROUNDS) as s:
                        sp.dma_start(own[:, :, 0:F], by_window(table[layer][bass.ds(s * NODES_R, NODES_R), :])
                                     ).then_inc(gen_own_in, 16)
                        sp.wait_ge(gen_scaled, layer * ROUNDS + s + 1)
                        sp.nop(nofuse=True)
                        sp.dma_start(by_window(base_table[layer][bass.ds(s * NODES_R, NODES_R), :]), z[:, :, 0:F]
                                     ).then_inc(gen_base_dma, 16)
                        sp.wait_ge(gen_base_dma, base0 + s * 16 + 16)
                        sp.nop(nofuse=True)
                    with sp.Fori(0, GEN_TILES) as i:
                        at = i * GEN_E
                        sp.dma_start(gen_src[:, :], src[bass.ds(at, GEN_E)].rearrange("(p o) -> p o", o=1)
                                     ).then_inc(gen_src_in, 16)
                        sp.dma_start(gen_dst[:, :], dst[bass.ds(at, GEN_E)].rearrange("(p o) -> p o", o=1)
                                     ).then_inc(gen_dst_in, 16)
                        sp.dma_start(gen_row[:, :], dst[bass.ds(at, GEN_E)].partition_broadcast(GEN_E)
                                     ).then_inc(gen_row_in, 16)
                        sp.wait_ge(gen_scattered, layer * 16 * GEN_TILES + i * 16 + 16)
                        sp.nop(nofuse=True)
                with sp.Else():
                    sp.nop()
                own_load(r0, layer)
                with sp.Fori(r0 + 1, r0 + ROUNDS) as r:
                    round_loads(r, layer, False)
                    sp.wait_ge(z_done, r * WINS)
                    sp.nop(nofuse=True)
                    own_load(r, layer)
                    if layer:
                        sp.wait_ge(z_done, r * WINS + 1)
                        sp.nop(nofuse=True)
                        sp.dma_start(resid[:, :, :],
                                     by_window(x[bass.ds(r * NODES_R - N_NODES - NODES_R, NODES_R), :])
                                     ).then_inc(resid_loaded, 16)
            sp.wait_ge(groups_summed, groups_after(2 * N_WIN - WINS))
            sp.dma_start(dst_idx[:, 0, :], dst_pad[N_EDGES:].rearrange("(p t) -> p t", t=TILES)
                         ).then_inc(dst_loaded[0], 16)
            sp.wait_ge(shift_ready, ROUNDS - 1)
            sp.dma_start(resid[:, :, :], by_window(x[N_NODES - NODES_R:N_NODES, :])).then_inc(resid_loaded, 16)

        @block_ctx.gpsimd
        def _(pool):
            pool.memset(dst_next, PAD_NODE).then_inc(tail_set, 1)
            pool.memset(pad_src[:, :], 0).then_inc(pads_set, 1)
            pool.memset(pad_dst[:, :], PAD_NODE).then_inc(pads_set, 1)
            pool.memset(ones[:, :], 1.0).then_inc(consts_set, 1)
            pool.iota(bound_i[:, :], pattern=[[0, 1]], base=0, channel_multiplier=NODES_W).then_inc(consts_set, 1)
            pool.iota(ids_i[:, :], pattern=[[1, NODES_W]], base=0, channel_multiplier=0).then_inc(consts_set, 1)
            pool.wait_ge(consts_set, 3)
            pool.affine_select(out=ident[:, :], in_=ones[:, :], compare_op=ALU.is_equal, fill=0.0, base=0,
                               pattern=[[-1, P]], channel_multiplier=1).then_inc(consts_set, 1)
            pool.affine_select(out=earlier[:, :], in_=ones[0:GEN_E, 0:GEN_E], compare_op=ALU.is_gt, fill=0.0,
                               base=0, pattern=[[-1, GEN_E]], channel_multiplier=1).then_inc(gen_mask, 1)
            pool.wait_ge(block_ready, 1)
            pool.indirect_dma_start(out=within[:, :], out_offset=None, in_=dst.rearrange("(a b) -> a b", b=SAMPLE),
                                    in_offset=bass.IndirectOffsetOnAxis(ap=block_i[:, 0:1], axis=0)
                                    ).then_inc(within_in, 16)
            general = load_flag(pool)

            for layer in range(2):
                F = F_TAB[layer]
                if layer:
                    pool.wait_ge(stored, 16 * ROUNDS)
                with pool.If(general):
                    with pool.Fori(0, GEN_TILES) as i:
                        for loaded in (gen_src_in, gen_dst_in):
                            pool.wait_ge(loaded, layer * 16 * GEN_TILES + i * 16 + 16)
                        pool.nop(nofuse=True)
                        for tile, tab, idx, landed in ((gen_in, table[layer], gen_src, gen_rows_in),
                                                       (gen_sum, base_table[layer], gen_dst, gen_sum_in)):
                            pool.indirect_dma_start(out=tile[:, 0:F], out_offset=None, in_=tab,
                                                    in_offset=bass.IndirectOffsetOnAxis(ap=idx[:, 0:1], axis=0)
                                                    ).then_inc(landed, 16)
                        pool.wait_ge(gen_new, layer * GEN_TILES + i + 1)
                        pool.nop(nofuse=True)
                        pool.indirect_dma_start(out=base_table[layer],
                                                out_offset=bass.IndirectOffsetOnAxis(ap=gen_to_i[:, 0:1], axis=0),
                                                in_=gen_sum[:, 0:F], in_offset=None,
                                                bounds_check=N_NODES - 1, oob_is_err=False
                                                ).then_inc(gen_scattered, 16)
                        pool.wait_ge(gen_scattered, layer * 16 * GEN_TILES + i * 16 + 16)
                with pool.Else():
                    pool.nop()

                def gather_window(w, j, r):
                    pool.wait_ge(src_loaded[j], 16 * r + 16)
                    for g, (t0, t1) in enumerate(GROUPS):
                        pool.wait_ge(groups_summed, w * NG + g + 1)
                        pool.nop(nofuse=True)
                        for t in range(t0, t1):
                            slot = (j % 2) * TILES + t
                            pool.indirect_dma_start(out=rows[:, slot, 0:F], out_offset=None, in_=table[layer],
                                                    in_offset=bass.IndirectOffsetOnAxis(ap=src_idx[:, j, t:t + 1], axis=0)
                                                    ).then_inc(rows_landed[slot], 16)

                with pool.Fori(layer * ROUNDS, layer * ROUNDS + ROUNDS) as r:
                    for j in range(WINS):
                        gather_window(r * WINS + j, j, r)

        @block_ctx.tensor
        def _(pe):
            pe.wait_ge(consts_set, 4)
            pe.wait_ge(first_ready, 2)
            nc.tensor.matmul(a_ps[0:1, 0, 0:N_BND], first[:, :], ident[0:N_BND, 0:N_BND], start=True, stop=True)
            nc.tensor.matmul(a_ps[0:1, 1, 0:1], unsorted[:, :], ones[0:SORT_P, 0:1], start=True, stop=True
                             ).then_inc(first_across, 1)
            pe.wait_ge(keep_ready, 1)
            nc.tensor.matmul(b_ps[0:NODES_W, 0, 0:1], ones[0:1, 0:NODES_W], flags[0:1, 4:5], start=True, stop=True
                             ).then_inc(keep_across, 1)
            general = load_flag(pe)
            pe.wait_ge(weights_in, 16 * 8)
            pe.sem_inc(groups_summed, CREDIT)

            for layer in range(2):
                F, K = F_TAB[layer], KB[layer]
                r0 = layer * ROUNDS
                with pe.If(general):
                    with pe.Fori(0, GEN_TILES) as i:
                        pe.wait_ge(gen_matrix, layer * GEN_TILES + i + 1)
                        pe.wait_ge(gen_rows_in, layer * 16 * GEN_TILES + i * 16 + 16)
                        nc.tensor.matmul(b_ps[0:GEN_E, 0, 0:F], gen_same[:, :], gen_in[:, 0:F], start=True, stop=True
                                         ).then_inc(gen_summed, 1)
                with pe.Else():
                    pe.nop()

                def sum_window(w, j, r, bank_waits=True):
                    pe.wait_ge(onehot_built, w + 1)
                    if bank_waits:
                        pe.wait_ge(z_done, w - 1)
                    for t0, t1 in GROUPS:
                        for t in range(t0, t1):
                            slot = (j % 2) * TILES + t
                            pe.wait_ge(rows_landed[slot], 16 * (2 * r + j // 2 + 1))
                            mm = nc.tensor.matmul(sum_ps[0:NODES_W, j % 2, 0:F], onehot[:, j % 2, t, :],
                                                  rows[:, slot, 0:F], start=(t == 0), stop=(t == TILES - 1))
                        mm.then_inc(groups_summed, 1)

                def transpose_round(q):
                    before = blocks_before(q, layer)
                    pe.wait_ge(z_done, q * WINS + WINS)
                    for k in range(K):
                        if k >= 2:
                            pe.wait_ge(t_read, before + k - 1)
                        for j in range(WINS):
                            mm = nc.tensor.transpose(t_ps[:, k % 2, j * NODES_W:(j + 1) * NODES_W],
                                                     z[:, j, k * P:(k + 1) * P], ident[0:NODES_W, 0:NODES_W])
                        mm.then_inc(t_ready, 1)

                def product(q, w, inT, blocks, done):
                    for m in range(MB):
                        if m >= 2:
                            pe.wait_ge(a_read, q * 2 * MB + done + m - 1)
                        for k in range(blocks):
                            mm = nc.tensor.matmul(a_ps[:, m % 2, 0:NODES_R], w[:, k, m * P:(m + 1) * P],
                                                  inT[:, k, :], start=(k == 0), stop=(k == blocks - 1))
                        mm.then_inc(a_ready, 1)

                def product_w1a(q):
                    pe.wait_ge(t_read, blocks_before(q, layer) + K)
                    product(q, w1a_s, zT, KB[0], 0)

                def product_w1b(q):
                    pe.wait_ge(a_read, q * 2 * MB + MB)
                    product(q, w1b_s, aT, MB, MB)

                def last_product(q, windows):
                    if layer:
                        pe.wait_ge(t_read, blocks_before(q, layer) + K)
                    else:
                        pe.wait_ge(a_read, q * 2 * MB + 2 * MB)
                    for j in windows:
                        if j >= 2:
                            pe.wait_ge(b_read, q * WINS + j - 1)
                        for k in range(MB):
                            mm = nc.tensor.matmul(b_ps[0:NODES_W, j % 2, 0:F_RES[layer]],
                                                  hT[:, k, j * NODES_W:(j + 1) * NODES_W], w_last[layer][:, k, :],
                                                  start=(k == 0), stop=(k == MB - 1))
                        mm.then_inc(b_ready, 1)

                for j in range(WINS):
                    sum_window(r0 * WINS + j, j, r0, bank_waits=(layer == 1 or j >= 2))
                with pe.Fori(r0 + 1, r0 + ROUNDS) as r:
                    q = r - 1
                    if layer == 0:
                        sum_window(r * WINS, 0, r)
                        transpose_round(q)
                        sum_window(r * WINS + 1, 1, r)
                        product_w1a(q)
                        sum_window(r * WINS + 2, 2, r)
                        product_w1b(q)
                        sum_window(r * WINS + 3, 3, r)
                        last_product(q, range(WINS))
                    else:
                        sum_window(r * WINS, 0, r)
                        transpose_round(q)
                        sum_window(r * WINS + 1, 1, r)
                        last_product(q, (0, 1))
                        sum_window(r * WINS + 2, 2, r)
                        last_product(q, (2, 3))
                        sum_window(r * WINS + 3, 3, r)
                q = r0 + ROUNDS - 1
                transpose_round(q)
                if layer == 0:
                    product_w1a(q)
                    product_w1b(q)
                pe.wait_ge(b_read, q * WINS)
                last_product(q, range(WINS))

        @block_ctx.scalar
        def _(act):
            with nc.allow_non_contiguous_dma(reason="biases to partitions, once"):
                for tile, w in ((w1a_s, w1a), (w1b_s, w1b), (w2a_s, w2a), (w2b_s, w2b)):
                    act.dma_start(tile[:, :, :], w.rearrange("(k p) n -> p k n", p=P)).then_inc(weights_in, 16)
                for tile, b in ((b1a_s, b1a), (b1b_s, b1b), (b2a_s, b2a)):
                    act.dma_start(tile[:, :], b.rearrange("(m p) -> p m", p=P)).then_inc(weights_in, 16)
                act.dma_start(b2b_s[:, :], b2b.partition_broadcast(NODES_W)).then_inc(weights_in, 16)
                for layer, e in enumerate((eps1, eps2)):
                    act.dma_start(eps[:, layer:layer + 1], e.partition_broadcast(NODES_W)).then_inc(eps_in, 16)
            act.wait_ge(weights_in, 16 * 8)

            for layer in range(2):
                r0 = layer * ROUNDS

                def dense_out(q):
                    before = blocks_before(q, layer)
                    for k in range(KB[layer]):
                        act.wait_ge(t_ready, before + k + 1)
                        if layer == 0:
                            nc.scalar.activation(zT[:, k, :], t_ps[:, k % 2, 0:NODES_R], ACT.Copy).then_inc(t_read, 1)
                        else:
                            nc.scalar.activation(hT[:, k, :], t_ps[:, k % 2, 0:NODES_R], ACT.Relu,
                                                 bias=b2a_s[:, k:k + 1]).then_inc(t_read, 1)
                    if layer == 0:
                        for n, (to, bias) in enumerate(((aT, b1a_s), (hT, b1b_s))):
                            for m in range(MB):
                                act.wait_ge(a_ready, q * 2 * MB + n * MB + m + 1)
                                nc.scalar.activation(to[:, m, :], a_ps[:, m % 2, 0:NODES_R], ACT.Relu,
                                                     bias=bias[:, m:m + 1]).then_inc(a_read, 1)
                        for j in range(WINS):
                            act.wait_ge(b_ready, q * WINS + j + 1)
                            nc.scalar.activation(staged[:, j, :], b_ps[0:NODES_W, j % 2, :], ACT.Copy
                                                 ).then_inc(b_read, 1)
                        act.wait_ge(b_read, q * WINS + WINS)
                    else:
                        act.wait_ge(var_ready, q - ROUNDS + 1)
                        nc.scalar.activation(std[:, :], var_eps[:, :], ACT.Sqrt).then_inc(std_ready, 1)
                        act.wait_ge(shift_ready, q - ROUNDS + 1)
                        for j in range(WINS):
                            nc.scalar.activation(staged[:, j, 0:F_OUT], staged[:, j, 0:F_OUT], ACT.Identity,
                                                 scale=rstd[:, j:j + 1], bias=shift[:, j:j + 1]
                                                 ).then_inc(staged_done, 1)
                        act.wait_ge(staged_done, (q - ROUNDS) * WINS + WINS)
                    node = q * NODES_R - layer * N_NODES
                    act.dma_start(result[layer][bass.ds(node, NODES_R), :].rearrange("(j p) f -> p j f", p=NODES_W),
                                  staged[:, :, 0:F_RES[layer]]).then_inc(stored, 16)
                    act.wait_ge(stored, q * 16 + 16)

                with act.Fori(r0, r0 + ROUNDS - 1) as q:
                    dense_out(q)
                dense_out(r0 + ROUNDS - 1)

        @block_ctx.vector
        def _(dve):
            steps = [0]

            def link(ins):
                steps[0] += 1
                ins.then_inc(dve_step, 1)
                dve.wait_ge(dve_step, steps[0])

            dve.wait_ge(consts_set, 3)
            link(nc.vector.tensor_copy(bound[:, :], bound_i[:, :]))
            nc.vector.tensor_copy(node_ids[:, :], ids_i[:, :])
            dve.wait_ge(sample_in, 16)
            link(nc.vector.tensor_scalar(below[:, 0:N_SAMP], sample[:, :], bound[:, 0:1], None, ALU.is_lt))
            link(nc.vector.tensor_reduce(out=count[:, 0:1], in_=below[:, 0:N_SAMP], axis=AX_X, op=ALU.add))
            link(nc.vector.tensor_scalar(block[:, :], count[:, 0:1], 1.0, 0.0, ALU.subtract, ALU.max))
            nc.vector.tensor_copy(block_i[:, :], block[:, :]).then_inc(block_ready, 1)
            dve.wait_ge(setup_dma, 48)
            link(nc.vector.tensor_tensor(falls, dst_here, dst_next, ALU.is_gt))
            nc.vector.tensor_reduce(out=unsorted[:, :], in_=falls, axis=AX_X, op=ALU.add).then_inc(first_ready, 1)
            dve.wait_ge(within_in, 16)
            link(nc.vector.tensor_scalar(below[:, :], within[:, :], bound[:, 0:1], None, ALU.is_lt))
            link(nc.vector.tensor_reduce(out=count[:, 1:2], in_=below[:, :], axis=AX_X, op=ALU.add))
            nc.vector.scalar_tensor_tensor(out=first[:, :], in0=block[:, :], scalar=float(SAMPLE), in1=count[:, 1:2],
                                           op0=ALU.mult, op1=ALU.add).then_inc(first_ready, 1)
            dve.wait_ge(first_across, 1)
            link(nc.vector.tensor_copy(first_row[:, :], a_ps[0:1, 0, 0:N_BND]))
            link(nc.vector.tensor_tensor(run_len[:, :], first_row[:, 1:N_BND], first_row[:, 0:N_WIN], ALU.subtract))
            link(nc.vector.tensor_reduce(out=flags[:, 0:1], in_=run_len[:, :], axis=AX_X, op=ALU.max))
            link(nc.vector.tensor_scalar(flags[:, 1:2], flags[:, 0:1], float(ROOM), None, ALU.is_gt))
            link(nc.vector.tensor_scalar(flags[:, 2:3], a_ps[0:1, 1, 0:1], 0.0, None, ALU.is_gt))
            link(nc.vector.tensor_tensor(flags[:, 3:4], flags[:, 1:2], flags[:, 2:3], ALU.max))
            link(nc.vector.tensor_scalar(flags[:, 4:5], flags[:, 3:4], -1.0, 1.0, ALU.mult, ALU.add))
            nc.vector.tensor_scalar(flags[:, 5:6], flags[:, 3:4], float(N_EDGES), None, ALU.mult).then_inc(keep_ready, 1)
            dve.wait_ge(keep_ready, 1)
            link(nc.vector.tensor_scalar(first_row[:, :], first_row[:, :], flags[:, 4:5], flags[:, 5:6],
                                         ALU.mult, ALU.add))
            link(nc.vector.tensor_copy(first_i[:, :], first_row[:, :]))
            nc.vector.tensor_copy(general_i[:, :], flags[:, 3:4]).then_inc(general_ready, 1)
            dve.wait_ge(eps_in, 32)
            dve.wait_ge(keep_across, 1)
            nc.vector.tensor_scalar(gen_scale[:, :], eps[:, :], 1.0, None, ALU.add)
            link(nc.vector.tensor_scalar(own_scale[:, :], eps[:, :], b_ps[0:NODES_W, 0, 0:1], 1.0, ALU.mult, ALU.add))
            general = load_flag(dve)
            dve.wait_ge(weights_in, 16 * 8)
            dve.wait_ge(gen_mask, 1)

            def build_onehot(w, slot, dst_slot, r):
                dve.wait_ge(dst_loaded[dst_slot], 16 * r + 16)
                nc.vector.tensor_tensor(
                    onehot[:, slot, :, :], dst_idx[:, dst_slot, :].unsqueeze(2).broadcast_to([P, TILES, NODES_W]),
                    node_ids[:, :].unsqueeze(1).broadcast_to([P, TILES, NODES_W]), ALU.is_equal
                    ).then_inc(onehot_built, 1)
                dve.wait_ge(onehot_built, w + 1)
                nc.vector.tensor_scalar(node_ids[:, :], node_ids[:, :], float(NODES_W), None, ALU.add
                                        ).then_inc(ids_moved, 1)
                dve.wait_ge(ids_moved, w + 1)
                if dst_slot == WINS - 1:
                    nc.vector.tensor_scalar(ids_over[:, :], node_ids[:, :], float(N_NODES), -float(N_NODES),
                                            ALU.is_ge, ALU.mult).then_inc(ids_wrapped, 1)
                    dve.wait_ge(ids_wrapped, 2 * r + 1)
                    nc.vector.tensor_tensor(node_ids[:, :], node_ids[:, :], ids_over[:, :], ALU.add
                                            ).then_inc(ids_wrapped, 1)
                    dve.wait_ge(ids_wrapped, 2 * r + 2)

            build_onehot(0, 0, 0, 0)

            for layer in range(2):
                F, FR = F_TAB[layer], F_RES[layer]
                r0 = layer * ROUNDS
                with dve.If(general):
                    with dve.Fori(0, ROUNDS) as s:
                        dve.wait_ge(gen_own_in, layer * 16 * ROUNDS + s * 16 + 16)
                        nc.vector.tensor_scalar(z[:, :, 0:F], own[:, :, 0:F], gen_scale[:, layer:layer + 1], None,
                                                ALU.mult).then_inc(gen_scaled, 1)
                    with dve.Fori(0, GEN_TILES) as i:
                        n = i + layer * GEN_TILES
                        dve.wait_ge(gen_dst_in, 16 * n + 16)
                        nc.vector.tensor_copy(gen_dst_f[:, :], gen_dst[:, :]).then_inc(gen_chain, 1)
                        dve.wait_ge(gen_chain, 5 * n + 1)
                        dve.wait_ge(gen_row_in, 16 * n + 16)
                        nc.vector.tensor_scalar(gen_same[:, :], gen_row[:, :], gen_dst_f[:, 0:1], None,
                                                ALU.is_equal).then_inc(gen_matrix, 1)
                        dve.wait_ge(gen_matrix, n + 1)
                        nc.vector.tensor_tensor(gen_before[:, :], gen_same[:, :], earlier[:, :], ALU.mult
                                                ).then_inc(gen_chain, 1)
                        dve.wait_ge(gen_chain, 5 * n + 2)
                        nc.vector.tensor_reduce(out=gen_dup[:, :], in_=gen_before[:, :], axis=AX_X, op=ALU.add
                                                ).then_inc(gen_chain, 1)
                        dve.wait_ge(gen_chain, 5 * n + 3)
                        nc.vector.scalar_tensor_tensor(out=gen_to[:, :], in0=gen_dup[:, :], scalar=float(N_NODES),
                                                       in1=gen_dst_f[:, :], op0=ALU.mult, op1=ALU.add
                                                       ).then_inc(gen_chain, 1)
                        dve.wait_ge(gen_chain, 5 * n + 4)
                        nc.vector.tensor_copy(gen_to_i[:, :], gen_to[:, :]).then_inc(gen_chain, 1)
                        dve.wait_ge(gen_chain, 5 * n + 5)
                        dve.wait_ge(gen_sum_in, 16 * n + 16)
                        dve.wait_ge(gen_summed, n + 1)
                        nc.vector.tensor_tensor(gen_sum[:, 0:F], gen_sum[:, 0:F], b_ps[0:GEN_E, 0, 0:F], ALU.add
                                                ).then_inc(gen_new, 1)
                with dve.Else():
                    dve.nop()

                def window_z(w, j, r, reused=True):
                    dve.wait_ge(groups_summed, groups_after(w))
                    dve.wait_ge(own_loaded, 16 * r + 16)
                    if reused:
                        dve.wait_ge(t_ready, blocks_before(r, layer))
                    nc.vector.scalar_tensor_tensor(out=z[:, j, 0:F], in0=own[:, j, 0:F],
                                                   scalar=own_scale[:, layer:layer + 1],
                                                   in1=sum_ps[0:NODES_W, j % 2, 0:F],
                                                   op0=ALU.mult, op1=ALU.add).then_inc(z_done, 1)

                def result_window(q, j):
                    v = q * WINS + j
                    dve.wait_ge(b_ready, v + 1)
                    y = staged[:, j, 0:FR]
                    n = v - N_WIN
                    nc.vector.tensor_tensor(y, b_ps[0:NODES_W, j % 2, 0:FR], b2b_s[:, :], ALU.add).then_inc(b_read, 1)
                    dve.wait_ge(b_read, v + 1)
                    dve.wait_ge(resid_loaded, (q - ROUNDS) * 16 + 16)
                    nc.vector.tensor_tensor(y, y, resid[:, j, :], ALU.add).then_inc(ln_chain, 1)
                    dve.wait_ge(ln_chain, 3 * n + 1)
                    nc.vector.bn_stats(out=stats[:, :], in_=y).then_inc(ln_chain, 1)
                    dve.wait_ge(ln_chain, 3 * n + 2)
                    dve.nop(nofuse=True)
                    nc.vector.bn_aggr(out=meanvar[:, j, :], in_=stats[:, :]).then_inc(ln_chain, 1)
                    dve.wait_ge(ln_chain, 3 * n + 3)

                def norm_factors(q):
                    n = q - ROUNDS
                    nc.vector.tensor_scalar(var_eps[:, :], meanvar[:, :, 1], LN_EPS, None, ALU.add
                                            ).then_inc(var_ready, 1)
                    dve.wait_ge(std_ready, n + 1)
                    nc.vector.reciprocal(rstd[:, :], std[:, :]).then_inc(rstd_ready, 1)
                    dve.wait_ge(rstd_ready, n + 1)
                    nc.vector.scalar_tensor_tensor(out=shift[:, :], in0=meanvar[:, :, 0], scalar=-1.0, in1=rstd[:, :],
                                                   op0=ALU.mult, op1=ALU.mult).then_inc(shift_ready, 1)

                def sums(r, j, reused=True):
                    w = r * WINS + j
                    if reused or j:
                        dve.wait_ge(groups_summed, groups_after(w - 1))
                    build_onehot(w + 1, (j + 1) % 2, (j + 1) % WINS, r + (j + 1) // WINS)
                    window_z(w, j, r, reused)

                for j in range(WINS):
                    sums(r0, j, reused=layer == 1)
                with dve.Fori(r0 + 1, r0 + ROUNDS) as r:
                    sums(r, 0)
                    sums(r, 1)
                    if layer:
                        result_window(r - 1, 0)
                        result_window(r - 1, 1)
                    sums(r, 2)
                    if layer:
                        result_window(r - 1, 2)
                        result_window(r - 1, 3)
                        norm_factors(r - 1)
                    sums(r, 3)
                if layer:
                    for j in range(WINS):
                        result_window(r0 + ROUNDS - 1, j)
                    norm_factors(r0 + ROUNDS - 1)


_INS = ['x', 'src', 'dst', 'L0_gnn_W1a', 'L0_gnn_b1a', 'L0_gnn_W1b', 'L0_gnn_b1b', 'L0_gnn_W2a', 'L0_gnn_b2a',
        'L0_gnn_W2b', 'L0_gnn_b2b', 'L0_gnn_eps1', 'L0_gnn_eps2']


def kernel(**inputs):
    import numpy as _np
    import concourse.bacc as _bacc
    from concourse import mybir as _mybir
    from concourse.bass_utils import run_bass_kernel_spmd as _run

    nc = _bacc.Bacc("TRN2", target_bir_lowering=False, num_devices=1)
    arrays, args = {}, []
    for name in _INS:
        a = _np.ascontiguousarray(inputs[name])
        if a.ndim == 0:
            a = a.reshape(1)
        arrays[f"in_{name}"] = a
        args.append(nc.dram_tensor(f"in_{name}", a.shape, _mybir.dt.from_np(a.dtype), kind="ExternalInput").ap())
    out = nc.dram_tensor("out", (N_NODES, F_OUT), _mybir.dt.float32, kind="ExternalOutput").ap()
    build(nc, *args, out)
    r = _run(nc, [arrays], core_ids=[0])
    return r.results[0]["out"]
```

```python
import concourse.bass as bass
from concourse import mybir
from contextlib import ExitStack

F32 = mybir.dt.float32
F32R = mybir.dt.float32r
I32 = mybir.dt.int32
ALU = mybir.AluOpType
ACT = mybir.ActivationFunctionType
AX_X = mybir.AxisListType.X

N_NODES, N_EDGES = 12500, 200000
F_IN, F_HID, F_OUT = 256, 512, 256
P = 128
WINS = 4
HALF = WINS // 2
NODES_H = HALF * P
TILES = 14
SPACING = TILES * P
ROUNDS = -(-N_EDGES // (SPACING * WINS))
N_WIN = ROUNDS * WINS
EDGE_ROOM = N_WIN * SPACING
EVEN = -(-N_NODES // N_WIN)
GROUPS = [[(0, 4), (4, 8), (8, 11), (11, TILES)], [(0, 3), (3, 6), (6, 10), (10, TILES)]]
SPLIT = [2, 2]
NG = len(GROUPS[0])
SPLIT_T = max(GROUPS[n][SPLIT[n] - 1][1] * (n + 1) for n in range(2))
RING = 2 * TILES
EARLY = 2
PAD_NODE = 1 << 23
N_CUT = N_WIN - 1
SORT_P = 125
SORT_F = N_EDGES // SORT_P
GEN_E = 125
GEN_TILES = N_EDGES // GEN_E
GEN_P = 125
GEN_R = GEN_P * WINS
GEN_ROUNDS = N_NODES // GEN_R
KB = [F_IN // P, F_HID // P]
MB = F_HID // P
F_TAB = [F_IN, F_HID]
F_RES = [F_HID, F_OUT]
LN_EPS = 1e-5
NO_NODE = 1 << 22


def build(nc, x, src, dst, src_tiles, dst_tiles, w1a, b1a, w1b, b1b, w2a, b2a, w2b, b2b, eps1, eps2, out):
    ctx = ExitStack()
    with ctx:
        def sb(name, shape, dt=F32):
            return ctx.enter_context(nc.sbuf_tensor(name, shape, dt))

        def sem(name):
            return ctx.enter_context(nc.semaphore(name))

        def scratch(name, shape, dt=F32):
            return nc.dram_tensor(name, shape, dt, kind="Internal").ap()

        hidden = scratch("hidden", [N_NODES + P, F_HID])
        base_table = [scratch("base_table1", [N_NODES + P, F_IN]), scratch("base_table2", [N_NODES + P, F_HID])]
        table = [x, hidden]

        rows = sb("rows", [P, RING, F_HID])
        onehot = sb("onehot", [P, 2, 1 + TILES, P], F32R)
        high = sb("high", [P, 2, SPLIT_T * F_IN], F32R)
        low = sb("low", [P, 2, SPLIT_T * F_IN], F32R)
        src_idx = sb("src_idx", [P, WINS, TILES], I32)
        dst_idx = sb("dst_idx", [P, WINS, 1 + TILES], I32)
        node_ids = sb("node_ids", [P, P])
        iota = sb("iota", [P, P])
        base_all = sb("base_all", [P, 2 * N_WIN + 1])
        own = sb("own", [P, WINS, F_HID])
        z = sb("z", [P, WINS, F_HID])
        zT = sb("zT", [P, KB[0], NODES_H])
        aT = sb("aT", [P, MB, NODES_H])
        hT = sb("hT", [P, MB, NODES_H])
        staged = sb("staged", [P, WINS, F_HID])
        resid = sb("resid", [P, WINS, F_OUT])
        w1a_s = sb("w1a_s", [P, KB[0], F_HID])
        w1b_s, w2a_s = (sb(n, [P, MB, F_HID]) for n in ("w1b_s", "w2a_s"))
        w2b_s = sb("w2b_s", [P, MB, F_OUT])
        w_last = [w2a_s, w2b_s]
        b1a_s, b1b_s, b2a_s = (sb(n, [P, MB]) for n in ("b1a_s", "b1b_s", "b2a_s"))
        b2b_s = sb("b2b_s", [P, F_OUT])
        ident = sb("ident", [P, P])
        ones = sb("ones", [P, P])
        eps = sb("eps", [P, 2])
        own_scale = sb("own_scale", [P, 2])
        gen_scale = sb("gen_scale", [P, 2])
        stats = sb("stats", [P, 6])
        meanvar = sb("meanvar", [P, HALF, 2])
        var_eps, std, rstd, shift = (sb(n, [P, HALF]) for n in ("var_eps", "std", "rstd", "shift"))
        cut_col_i = sb("cut_col_i", [N_CUT, 1], I32)
        cut_col = sb("cut_col", [N_CUT, 1])
        before_cut = sb("before_cut", [N_CUT, P], I32)
        same_node = sb("same_node", [N_CUT, P])
        back = sb("back", [N_CUT, 1])
        unsorted = sb("unsorted", [SORT_P, 1])
        cut_row_i = sb("cut_row_i", [1, N_CUT], I32)
        node_row = sb("node_row", [1, N_WIN + 1])
        ids_row = sb("ids_row", [1, N_WIN])
        even_i = sb("even_i", [1, N_WIN + 1], I32)
        even = sb("even", [1, N_WIN + 1])
        span = sb("span", [1, N_WIN])
        flags = sb("flags", [1, 16])
        base_i = sb("base_i", [1, N_WIN + 1], I32)
        general_i = sb("general_i", [1, 1], I32)
        ids_i = sb("ids_i", [P, P], I32)
        own_flat, z_flat, staged_flat = (t[:, :, :].rearrange("p a b -> p (a b)") for t in (own, z, staged))
        dst_here = own_flat[0:SORT_P, 0:SORT_F].bitcast(I32)
        dst_next = z_flat[0:SORT_P, 0:SORT_F].bitcast(I32)
        falls = staged_flat[0:SORT_P, 0:SORT_F]
        gen_src = sb("gen_src", [GEN_E, 1], I32)
        gen_dst = sb("gen_dst", [GEN_E, 1], I32)
        gen_row = sb("gen_row", [GEN_E, GEN_E], I32)
        gen_dst_f = sb("gen_dst_f", [GEN_E, 1])
        gen_same = sb("gen_same", [GEN_E, GEN_E])
        gen_before = sb("gen_before", [GEN_E, GEN_E])
        earlier = sb("earlier", [GEN_E, GEN_E])
        gen_dup = sb("gen_dup", [GEN_E, 1])
        gen_to = sb("gen_to", [GEN_E, 1])
        gen_to_i = sb("gen_to_i", [GEN_E, 1], I32)
        gen_rows = aT[:, :, :].rearrange("p a b -> p (a b)")
        gen_in, gen_sum = gen_rows[0:GEN_E, 0:F_HID], gen_rows[0:GEN_E, F_HID:2 * F_HID]

        def banks(name):
            return ctx.enter_context(nc.psum_tensor(name, [P, 2, 512], F32))
        sum_ps, t_ps, a_ps, b_ps = banks("sum_ps"), banks("t_ps"), banks("a_ps"), banks("b_ps")

        setup_dma = sem("setup_dma")
        cuts_in = sem("cuts_in")
        weights_in = sem("weights_in")
        eps_in = sem("eps_in")
        consts_set = sem("consts_set")
        first_ready = sem("first_ready")
        first_across = sem("first_across")
        keep_ready = sem("keep_ready")
        keep_across = sem("keep_across")
        general_ready = sem("general_ready")
        src_loaded = [sem(f"src_loaded{j}") for j in range(WINS)]
        dst_loaded = [sem(f"dst_loaded{j}") for j in range(WINS)]
        own_loaded = sem("own_loaded")
        resid_loaded = sem("resid_loaded")
        rows_landed = [sem(f"rows_landed{t}") for t in range(RING)]
        onehot_built = sem("onehot_built")
        groups_summed = sem("groups_summed")
        shared_used = sem("shared_used")
        high_done = sem("high_done")
        low_done = sem("low_done")
        z_done = sem("z_done")
        t_ready = sem("t_ready")
        t_read = sem("t_read")
        a_ready = sem("a_ready")
        a_read = sem("a_read")
        b_ready = sem("b_ready")
        b_read = sem("b_read")
        staged_done = sem("staged_done")
        var_ready = sem("var_ready")
        std_ready = sem("std_ready")
        rstd_ready = sem("rstd_ready")
        shift_ready = sem("shift_ready")
        stored = sem("stored")
        dve_step = sem("dve_step")
        gen_own_in = sem("gen_own_in")
        gen_src_in = sem("gen_src_in")
        gen_dst_in = sem("gen_dst_in")
        gen_row_in = sem("gen_row_in")
        gen_scaled = sem("gen_scaled")
        gen_base_dma = sem("gen_base_dma")
        gen_pad_dma = sem("gen_pad_dma")
        gen_rows_in = sem("gen_rows_in")
        gen_sum_in = sem("gen_sum_in")
        gen_matrix = sem("gen_matrix")
        gen_summed = sem("gen_summed")
        gen_new = sem("gen_new")
        gen_scattered = sem("gen_scattered")
        gen_mask = sem("gen_mask")
        gen_chain = sem("gen_chain")
        ids_ready = sem("ids_ready")
        base_across = sem("base_across")
        base_ready = sem("base_ready")
        ln_chain = sem("ln_chain")

        CREDIT = 2 * NG
        LOW_CREDIT = 2 * SPLIT[0]

        def split_before(w, layer):
            return w * SPLIT[layer] + layer * N_WIN * (SPLIT[0] - SPLIT[1])

        def part(tile, layer, j, t0, t1):
            F = F_TAB[layer]
            return tile[:, j % 2, t0 * F:t1 * F]

        def groups_after(w):
            return w * NG + NG + CREDIT

        def blocks_before(h, layer):
            return h * KB[layer] - layer * 2 * ROUNDS * (KB[1] - KB[0])

        def resid_batches(r):
            return 16 * (WINS * r - (WINS * ROUNDS - HALF))

        def load_flag(eng):
            eng.wait_ge(general_ready, 1)
            return eng.value_load(general_i[0:1, 0:1], min_val=0, max_val=1)

        block_ctx = ctx.enter_context(nc.Block())

        @block_ctx.sync
        def _(sp):
            def load_src(w, j):
                sp.dma_start(src_idx[:, j, :], src_tiles[:, bass.ds(w * TILES, TILES)]).then_inc(src_loaded[j], 16)

            def load_dst(w, j):
                sp.dma_start(dst_idx[:, j, :], dst_tiles[:, bass.ds(w * TILES, 1 + TILES)]).then_inc(dst_loaded[j], 16)

            for j in range(EARLY):
                load_src(j, j)
            for tile, at in ((dst_here, 0), (dst_next, 1)):
                sp.dma_start(tile, dst[at:at + N_EDGES].rearrange("(p f) -> p f", p=SORT_P)).then_inc(setup_dma, 16)
            with nc.allow_non_contiguous_dma(reason="one node of each window"):
                at_cuts = dst[SPACING:SPACING + (N_CUT - 1) * SPACING + 1:SPACING]
                sp.dma_start(cut_col_i[:, :], at_cuts.rearrange("(a b) -> a b", b=1)).then_inc(cuts_in, 16)
                sp.dma_start(cut_row_i[:, :], at_cuts.rearrange("(a b) -> a b", a=1)).then_inc(cuts_in, 16)
            sp.dma_start(before_cut[:, :], dst[SPACING - P:SPACING - P + N_CUT * SPACING]
                         .rearrange("(w s) -> w s", s=SPACING)[:, 0:P]).then_inc(cuts_in, 16)
            general = load_flag(sp)

            def load_nodes(tile, F, tab, v, windows, layer, loaded):
                for j in windows:
                    node = sp.value_load(base_i[0:1, bass.ds(v + j - layer * N_WIN, 1)],
                                         min_val=0, max_val=N_NODES)
                    sp.dma_start(tile[:, j % WINS, 0:F], tab[bass.ds(node, P), :]).then_inc(loaded, 16)

            def by_part(rows_ap):
                return rows_ap.rearrange("(j p) f -> p j f", p=GEN_P)

            def round_loads(r, layer, first_round, windows):
                for j in windows:
                    if not (layer == 0 and first_round):
                        sp.wait_ge(groups_summed, groups_after((r - 1) * WINS + j))
                        sp.nop(nofuse=True)
                    if not (layer == 0 and first_round and j < EARLY):
                        load_src(r * WINS + j - layer * N_WIN, j)
                    load_dst(r * WINS + j - layer * N_WIN, j)

            def own_load(r, layer):
                with sp.If(general):
                    load_nodes(own, F_TAB[layer], base_table[layer], r * WINS, range(WINS), layer, own_loaded)
                with sp.Else():
                    load_nodes(own, F_TAB[layer], table[layer], r * WINS, range(WINS), layer, own_loaded)

            def store_windows(q, windows, layer, first=False):
                done, to = (b_read, hidden) if layer == 0 else (staged_done, out)
                for j in windows:
                    sp.wait_ge(done, q * WINS + j + 1 - layer * N_WIN)
                    sp.nop(nofuse=True)
                    if not (first and j == 0):
                        sp.wait_ge(stored, (q * WINS + j) * 16)
                        sp.nop(nofuse=True)
                    node = sp.value_load(base_i[0:1, bass.ds(q * WINS + j - layer * N_WIN, 1)],
                                         min_val=0, max_val=N_NODES)
                    sp.dma_start(to[bass.ds(node, P), :], staged[:, j, 0:F_RES[layer]]).then_inc(stored, 16)

            for layer in range(2):
                F = F_TAB[layer]
                r0 = layer * ROUNDS
                round_loads(r0, layer, True, (0, 1))
                if layer:
                    store_windows(ROUNDS - 2, (2, 3), 0)
                round_loads(r0, layer, True, (2, 3))
                if layer:
                    store_windows(ROUNDS - 1, range(WINS), 0)
                    sp.wait_ge(stored, 16 * N_WIN)
                    sp.wait_ge(z_done, r0 * WINS)
                    sp.nop(nofuse=True)
                with sp.If(general):
                    with sp.Fori(0, GEN_ROUNDS) as s:
                        sp.dma_start(own[0:GEN_P, :, 0:F], by_part(table[layer][bass.ds(s * GEN_R, GEN_R), :])
                                     ).then_inc(gen_own_in, 16)
                        sp.wait_ge(gen_scaled, layer * GEN_ROUNDS + s + 1)
                        sp.nop(nofuse=True)
                        sp.dma_start(by_part(base_table[layer][bass.ds(s * GEN_R, GEN_R), :]), z[0:GEN_P, :, 0:F]
                                     ).then_inc(gen_base_dma, 16)
                        sp.wait_ge(gen_base_dma, layer * 16 * GEN_ROUNDS + s * 16 + 16)
                        sp.nop(nofuse=True)
                    for c in range(0, F, F_IN):
                        sp.dma_start(base_table[layer][N_NODES:, c:c + F_IN], x[N_NODES:, :]).then_inc(gen_pad_dma, 16)
                    sp.wait_ge(gen_pad_dma, 16 if layer == 0 else 16 + 16 * F_HID // F_IN)
                    with sp.Fori(0, GEN_TILES) as i:
                        at = i * GEN_E
                        sp.dma_start(gen_src[:, :], src[bass.ds(at, GEN_E)].rearrange("(p o) -> p o", o=1)
                                     ).then_inc(gen_src_in, 16)
                        sp.dma_start(gen_dst[:, :], dst[bass.ds(at, GEN_E)].rearrange("(p o) -> p o", o=1)
                                     ).then_inc(gen_dst_in, 16)
                        sp.dma_start(gen_row[:, :], dst[bass.ds(at, GEN_E)].partition_broadcast(GEN_E)
                                     ).then_inc(gen_row_in, 16)
                        sp.wait_ge(gen_scattered, layer * 16 * GEN_TILES + i * 16 + 16)
                        sp.nop(nofuse=True)
                with sp.Else():
                    sp.nop()
                own_load(r0, layer)
                if layer:
                    load_nodes(resid, F_OUT, x, r0 * WINS, (0, 1), layer, resid_loaded)

                def round_steps(r, first):
                    round_loads(r, layer, False, (0, 1))
                    if not first:
                        store_windows(r - 2, (2, 3), layer)
                    round_loads(r, layer, False, (2, 3))
                    sp.wait_ge(z_done, r * WINS)
                    sp.nop(nofuse=True)
                    own_load(r, layer)
                    store_windows(r - 1, (0, 1), layer, first=first and layer == 0)
                    if layer:
                        sp.wait_ge(z_done, r * WINS + 1)
                        sp.nop(nofuse=True)
                        load_nodes(resid, F_OUT, x, (r - 1) * WINS, range(2, 2 + WINS), layer, resid_loaded)

                round_steps(r0 + 1, True)
                with sp.Fori(r0 + 2, r0 + ROUNDS) as r:
                    round_steps(r, False)
            sp.wait_ge(groups_summed, groups_after(2 * N_WIN - WINS))
            sp.dma_start(dst_idx[:, 0, :], dst_tiles[:, 0:1 + TILES]).then_inc(dst_loaded[0], 16)
            store_windows(2 * ROUNDS - 2, (2, 3), 1)
            sp.wait_ge(z_done, 2 * N_WIN - 1)
            load_nodes(resid, F_OUT, x, 2 * N_WIN - WINS, (2, 3), 1, resid_loaded)
            store_windows(2 * ROUNDS - 1, range(WINS), 1)
            sp.wait_ge(stored, 16 * 2 * N_WIN)

        @block_ctx.gpsimd
        def _(pool):
            def gather_window(layer, w, j, r):
                pool.wait_ge(src_loaded[j], 16 * r + 16)
                for g, (t0, t1) in enumerate(GROUPS[layer]):
                    if g < SPLIT[layer]:
                        pool.wait_ge(low_done, split_before(w, layer) - 2 * SPLIT[layer] + g + 1 + LOW_CREDIT)
                    else:
                        pool.wait_ge(groups_summed, w * NG + g - SPLIT[layer] + 1)
                    if g == NG - 1:
                        pool.nop(nofuse=True)
                        pool.wait_ge(shared_used, w + 1 - layer)
                    pool.nop(nofuse=True)
                    for t in range(t0, t1):
                        slot = (j % 2) * TILES + t
                        pool.indirect_dma_start(out=rows[:, slot, 0:F_TAB[layer]], out_offset=None, in_=table[layer][0:N_NODES, :],
                                                in_offset=bass.IndirectOffsetOnAxis(ap=src_idx[:, j, t:t + 1], axis=0)
                                                ).then_inc(rows_landed[slot], 16)

            pool.memset(ones[:, :], 1.0).then_inc(consts_set, 1)
            pool.iota(even_i[:, :], pattern=[[EVEN, N_WIN + 1]], base=0, channel_multiplier=0).then_inc(consts_set, 1)
            pool.iota(ids_i[:, :], pattern=[[1, P]], base=0, channel_multiplier=0).then_inc(consts_set, 1)
            pool.wait_ge(consts_set, 3)
            pool.affine_select(out=ident[:, :], in_=ones[:, :], compare_op=ALU.is_equal, fill=0.0, base=0,
                               pattern=[[-1, P]], channel_multiplier=1).then_inc(consts_set, 1)
            pool.affine_select(out=earlier[:, :], in_=ones[0:GEN_E, 0:GEN_E], compare_op=ALU.is_gt, fill=0.0,
                               base=0, pattern=[[-1, GEN_E]], channel_multiplier=1).then_inc(gen_mask, 1)
            for j in range(EARLY):
                gather_window(0, j, j, 0)
            general = load_flag(pool)

            for layer in range(2):
                F = F_TAB[layer]
                if layer:
                    pool.wait_ge(stored, 16 * N_WIN)
                with pool.If(general):
                    with pool.Fori(0, GEN_TILES) as i:
                        for loaded in (gen_src_in, gen_dst_in):
                            pool.wait_ge(loaded, layer * 16 * GEN_TILES + i * 16 + 16)
                        pool.nop(nofuse=True)
                        for tile, tab, idx, landed in ((gen_in, table[layer], gen_src, gen_rows_in),
                                                       (gen_sum, base_table[layer], gen_dst, gen_sum_in)):
                            pool.indirect_dma_start(out=tile[:, 0:F], out_offset=None, in_=tab[0:N_NODES, :],
                                                    in_offset=bass.IndirectOffsetOnAxis(ap=idx[:, 0:1], axis=0)
                                                    ).then_inc(landed, 16)
                        pool.wait_ge(gen_new, layer * GEN_TILES + i + 1)
                        pool.nop(nofuse=True)
                        pool.indirect_dma_start(out=base_table[layer][0:N_NODES, :],
                                                out_offset=bass.IndirectOffsetOnAxis(ap=gen_to_i[:, 0:1], axis=0),
                                                in_=gen_sum[:, 0:F], in_offset=None,
                                                bounds_check=N_NODES - 1, oob_is_err=False
                                                ).then_inc(gen_scattered, 16)
                        pool.wait_ge(gen_scattered, layer * 16 * GEN_TILES + i * 16 + 16)
                with pool.Else():
                    pool.nop()

                first = layer * ROUNDS
                for j in range(EARLY if layer == 0 else 0, WINS):
                    gather_window(layer, first * WINS + j, j, first)
                with pool.Fori(first + 1, first + ROUNDS) as r:
                    for j in range(WINS):
                        gather_window(layer, r * WINS + j, j, r)

        @block_ctx.tensor
        def _(pe):
            pe.sem_inc(groups_summed, CREDIT)
            pe.sem_inc(low_done, LOW_CREDIT)
            pe.sem_inc(shared_used, 2)
            pe.wait_ge(consts_set, 4)
            pe.wait_ge(first_ready, 2)
            nc.tensor.matmul(a_ps[0:1, 0, 0:N_CUT], back[:, :], ident[0:N_CUT, 0:N_CUT], start=True, stop=True)
            nc.tensor.matmul(a_ps[0:1, 1, 0:1], unsorted[:, :], ones[0:SORT_P, 0:1], start=True, stop=True
                             ).then_inc(first_across, 1)
            pe.wait_ge(keep_ready, 1)
            nc.tensor.matmul(b_ps[:, 0, 0:1], ones[0:1, :], flags[0:1, 8:9], start=True, stop=True
                             ).then_inc(keep_across, 1)
            pe.wait_ge(base_ready, 1)
            nc.tensor.matmul(b_ps[:, 1, 0:N_WIN], ones[0:1, :], ids_row[:, :], start=True, stop=True
                             ).then_inc(base_across, 1)
            general = load_flag(pe)

            for layer in range(2):
                F, K = F_TAB[layer], KB[layer]
                r0 = layer * ROUNDS
                with pe.If(general):
                    with pe.Fori(0, GEN_TILES) as i:
                        pe.wait_ge(gen_matrix, layer * GEN_TILES + i + 1)
                        pe.wait_ge(gen_rows_in, layer * 16 * GEN_TILES + i * 16 + 16)
                        nc.tensor.matmul(b_ps[0:GEN_E, 0, 0:F], gen_same[:, :], gen_in[:, 0:F], start=True, stop=True
                                         ).then_inc(gen_summed, 1)
                with pe.Else():
                    pe.nop()

                def sum_window(w, j, r, bank_waits=True, shared=True):
                    pe.wait_ge(onehot_built, w + 1)
                    if bank_waits:
                        pe.wait_ge(z_done, w - 1)
                    into = sum_ps[:, j % 2, 0:F]
                    if shared:
                        slot = ((j + 1) % 2) * TILES + TILES - 1
                        nc.tensor.matmul(into, onehot[:, j % 2, 0, :].bitcast(F32), rows[:, slot, 0:F],
                                         start=True, stop=False).then_inc(shared_used, 1)
                    n_split = SPLIT[layer]
                    groups = GROUPS[layer]
                    for t0, t1 in groups[n_split:]:
                        for t in range(t0, t1):
                            slot = (j % 2) * TILES + t
                            pe.wait_ge(rows_landed[slot], 16 * (2 * r + j // 2 + 1))
                            mm = nc.tensor.matmul(into, onehot[:, j % 2, 1 + t, :].bitcast(F32), rows[:, slot, 0:F],
                                                  start=(t == groups[n_split][0] and not shared), stop=False)
                        mm.then_inc(groups_summed, 1)
                    for g in range(n_split):
                        pe.wait_ge(low_done, split_before(w, layer) + g + 1 + LOW_CREDIT)
                        for t in range(*groups[g]):
                            for n, tile in enumerate((high, low)):
                                last = n == 1 and g == n_split - 1 and t == groups[g][1] - 1
                                mm = nc.tensor.matmul(into, onehot[:, j % 2, 1 + t, :],
                                                      part(tile, layer, j, t, t + 1), start=False, stop=last)
                        mm.then_inc(groups_summed, 1)

                def transpose_half(h, j0):
                    before = blocks_before(h, layer)
                    pe.wait_ge(z_done, h * HALF + HALF)
                    for k in range(K):
                        if k >= 2:
                            pe.wait_ge(t_read, before + k - 1)
                        for j in range(HALF):
                            mm = nc.tensor.transpose(t_ps[:, k % 2, j * P:(j + 1) * P],
                                                     z[:, j0 + j, k * P:(k + 1) * P], ident[:, :])
                        mm.then_inc(t_ready, 1)

                def product(h, w, inT, blocks, done):
                    for m in range(MB):
                        if m >= 2:
                            pe.wait_ge(a_read, h * 2 * MB + done + m - 1)
                        for k in range(blocks):
                            mm = nc.tensor.matmul(a_ps[:, m % 2, 0:NODES_H], w[:, k, m * P:(m + 1) * P],
                                                  inT[:, k, :], start=(k == 0), stop=(k == blocks - 1))
                        mm.then_inc(a_ready, 1)

                def first_products(h):
                    pe.wait_ge(t_read, blocks_before(h, layer) + K)
                    product(h, w1a_s, zT, KB[0], 0)
                    pe.wait_ge(a_read, h * 2 * MB + MB)
                    product(h, w1b_s, aT, MB, MB)

                def last_product(h, reused=True):
                    if layer:
                        pe.wait_ge(t_read, blocks_before(h, layer) + K)
                    else:
                        pe.wait_ge(a_read, h * 2 * MB + 2 * MB)
                    for j in range(HALF):
                        if reused:
                            pe.wait_ge(b_read, h * HALF + j - 1)
                        for k in range(MB):
                            mm = nc.tensor.matmul(b_ps[0:P, j, 0:F_RES[layer]],
                                                  hT[:, k, j * P:(j + 1) * P], w_last[layer][:, k, :],
                                                  start=(k == 0), stop=(k == MB - 1))
                        mm.then_inc(b_ready, 1)

                first_h = layer * 2 * ROUNDS
                for j in range(WINS):
                    if j == 2 and layer == 0:
                        transpose_half(first_h, 0)
                    if j == 3:
                        if layer == 0:
                            pe.wait_ge(weights_in, 16 * 8)
                            first_products(first_h)
                        else:
                            transpose_half(first_h, 0)
                    sum_window(r0 * WINS + j, j, r0, bank_waits=(layer == 1 or j >= 2), shared=(j > 0))
                last_product(first_h, reused=layer == 1)
                with pe.Fori(r0 + 1, r0 + ROUNDS) as r:
                    for h, j0 in ((2 * r - 1, 2), (2 * r, 0)):
                        j = 2 - j0
                        if layer == 0:
                            transpose_half(h, j0)
                            sum_window(r * WINS + j, j, r)
                            first_products(h)
                        else:
                            sum_window(r * WINS + j, j, r)
                            transpose_half(h, j0)
                        sum_window(r * WINS + j + 1, j + 1, r)
                        last_product(h)
                h = 2 * (r0 + ROUNDS) - 1
                transpose_half(h, 2)
                if layer == 0:
                    first_products(h)
                last_product(h)

        @block_ctx.scalar
        def _(act):
            for layer, e in enumerate((eps1, eps2)):
                act.dma_start(eps[:, layer:layer + 1], e.partition_broadcast(P)).then_inc(eps_in, 16)
            act.wait_ge(general_ready, 1)
            with nc.allow_non_contiguous_dma(reason="biases to partitions, once"):
                for tile, w in ((w1a_s, w1a), (w1b_s, w1b), (w2a_s, w2a), (w2b_s, w2b)):
                    act.dma_start(tile[:, :, :], w.rearrange("(k p) n -> p k n", p=P)).then_inc(weights_in, 16)
                for tile, b in ((b1a_s, b1a), (b1b_s, b1b), (b2a_s, b2a)):
                    act.dma_start(tile[:, :], b.rearrange("(m p) -> p m", p=P)).then_inc(weights_in, 16)
                act.dma_start(b2b_s[:, :], b2b.partition_broadcast(P)).then_inc(weights_in, 16)

            for layer in range(2):
                r0 = layer * ROUNDS

                def split_high(w, j, r):
                    act.wait_ge(groups_summed, groups_after(w) - 2 * NG)
                    for g in range(SPLIT[layer]):
                        t0, t1 = GROUPS[layer][g]
                        slot = (j % 2) * TILES
                        for t in range(t0, t1):
                            act.wait_ge(rows_landed[slot + t], 16 * (2 * r + j // 2 + 1))
                        nc.scalar.activation(
                            part(high, layer, j, t0, t1).rearrange("p (t f) -> p t f", t=t1 - t0),
                            rows[:, slot + t0:slot + t1, 0:F_TAB[layer]], ACT.Copy).then_inc(high_done, 1)

                def copy_transposes(h):
                    before = blocks_before(h, layer)
                    for k in range(KB[layer]):
                        act.wait_ge(t_ready, before + k + 1)
                        if layer == 0:
                            nc.scalar.activation(zT[:, k, :], t_ps[:, k % 2, 0:NODES_H], ACT.Copy).then_inc(t_read, 1)
                        else:
                            nc.scalar.activation(hT[:, k, :], t_ps[:, k % 2, 0:NODES_H], ACT.Relu,
                                                 bias=b2a_s[:, k:k + 1]).then_inc(t_read, 1)

                def relu_products(h):
                    for to, bias, done in ((aT, b1a_s, 0), (hT, b1b_s, MB)):
                        for m in range(MB):
                            act.wait_ge(a_ready, h * 2 * MB + done + m + 1)
                            nc.scalar.activation(to[:, m, :], a_ps[:, m % 2, 0:NODES_H], ACT.Relu,
                                                 bias=bias[:, m:m + 1]).then_inc(a_read, 1)

                def copy_products(h, j0, reused=True):
                    if reused:
                        act.wait_ge(stored, 16 * (h * HALF - HALF))
                    for j in range(HALF):
                        act.wait_ge(b_ready, h * HALF + j + 1)
                        nc.scalar.activation(staged[:, j0 + j, :], b_ps[:, j, :], ACT.Copy).then_inc(b_read, 1)

                def normalize(h, j0):
                    n = h - 2 * ROUNDS
                    act.wait_ge(var_ready, n + 1)
                    nc.scalar.activation(std[:, :], var_eps[:, :], ACT.Sqrt).then_inc(std_ready, 1)
                    act.wait_ge(shift_ready, n + 1)
                    for j in range(HALF):
                        y = staged[:, j0 + j, 0:F_OUT]
                        nc.scalar.activation(y, y, ACT.Identity, scale=rstd[:, j:j + 1], bias=shift[:, j:j + 1]
                                             ).then_inc(staged_done, 1)

                first_h = layer * 2 * ROUNDS
                split_high(r0 * WINS, 0, r0)
                split_high(r0 * WINS + 1, 1, r0)
                if layer == 0:
                    copy_transposes(first_h)
                    split_high(r0 * WINS + 2, 2, r0)
                    act.wait_ge(weights_in, 16 * 8)
                    relu_products(first_h)
                    split_high(r0 * WINS + 3, 3, r0)
                    copy_products(first_h, 0, reused=False)
                else:
                    split_high(r0 * WINS + 2, 2, r0)
                    copy_transposes(first_h)
                    split_high(r0 * WINS + 3, 3, r0)
                    normalize(first_h, 0)
                with act.Fori(r0 + 1, r0 + ROUNDS) as r:
                    for h, j0 in ((2 * r - 1, 2), (2 * r, 0)):
                        j = 2 - j0
                        if layer == 0:
                            copy_transposes(h)
                            split_high(r * WINS + j, j, r)
                            relu_products(h)
                            split_high(r * WINS + j + 1, j + 1, r)
                            copy_products(h, j0)
                        else:
                            split_high(r * WINS + j, j, r)
                            copy_transposes(h)
                            split_high(r * WINS + j + 1, j + 1, r)
                            normalize(h, j0)
                h = 2 * (r0 + ROUNDS) - 1
                copy_transposes(h)
                if layer == 0:
                    relu_products(h)
                    copy_products(h, 2)
                else:
                    normalize(h, 2)

        @block_ctx.vector
        def _(dve):
            steps = [0]

            def link(ins):
                steps[0] += 1
                ins.then_inc(dve_step, 1)
                dve.wait_ge(dve_step, steps[0])

            dve.wait_ge(consts_set, 3)
            link(nc.vector.tensor_copy(iota[:, :], ids_i[:, :]))
            link(nc.vector.tensor_copy(even[:, :], even_i[:, :]))
            dve.wait_ge(cuts_in, 48)
            link(nc.vector.tensor_copy(cut_col[:, :], cut_col_i[:, :]))
            link(nc.vector.tensor_scalar(same_node[:, :], before_cut[:, :], cut_col[:, 0:1], None, ALU.is_equal))
            nc.vector.tensor_reduce(out=back[:, :], in_=same_node[:, :], axis=AX_X, op=ALU.add).then_inc(first_ready, 1)
            link(nc.vector.memset(node_row[:, 0:1], 0.0))
            link(nc.vector.tensor_copy(node_row[:, 1:N_WIN], cut_row_i[:, :]))
            link(nc.vector.memset(node_row[:, N_WIN:N_WIN + 1], float(N_NODES)))
            link(nc.vector.tensor_tensor(span[:, :], node_row[:, 1:N_WIN + 1], node_row[:, 0:N_WIN], ALU.subtract))
            dve.wait_ge(setup_dma, 32)
            link(nc.vector.tensor_tensor(falls, dst_here, dst_next, ALU.is_gt))
            nc.vector.tensor_reduce(out=unsorted[:, :], in_=falls, axis=AX_X, op=ALU.add).then_inc(first_ready, 1)
            dve.wait_ge(first_across, 1)
            for f, (row, most) in enumerate(((span[:, :], P), (a_ps[0:1, 0, 0:N_CUT], P - 1))):
                link(nc.vector.tensor_reduce(out=flags[:, f:f + 1], in_=row, axis=AX_X, op=ALU.max))
                link(nc.vector.tensor_scalar(flags[:, f + 5:f + 6], flags[:, f:f + 1], float(most), None, ALU.is_gt))
            link(nc.vector.tensor_scalar(flags[:, 7:8], a_ps[0:1, 1, 0:1], 0.0, None, ALU.is_gt))
            link(nc.vector.tensor_reduce(out=flags[:, 3:4], in_=flags[:, 5:8], axis=AX_X, op=ALU.max))
            link(nc.vector.tensor_scalar(flags[:, 8:9], flags[:, 3:4], -1.0, 1.0, ALU.mult, ALU.add))
            nc.vector.tensor_scalar(flags[:, 9:10], flags[:, 3:4], float(NO_NODE), None, ALU.mult).then_inc(keep_ready, 1)
            dve.wait_ge(keep_ready, 1)
            link(nc.vector.tensor_scalar(even[:, :], even[:, :], flags[:, 3:4], None, ALU.mult))
            link(nc.vector.scalar_tensor_tensor(out=node_row[:, :], in0=node_row[:, :], scalar=flags[:, 8:9],
                                                in1=even[:, :], op0=ALU.mult, op1=ALU.add))
            nc.vector.tensor_scalar(ids_row[:, :], node_row[:, 0:N_WIN], flags[:, 9:10], None, ALU.add
                                    ).then_inc(base_ready, 1)
            link(nc.vector.tensor_copy(base_i[:, :], node_row[:, :]))
            nc.vector.tensor_copy(general_i[:, :], flags[:, 3:4]).then_inc(general_ready, 1)
            dve.wait_ge(eps_in, 32)
            dve.wait_ge(keep_across, 1)
            nc.vector.tensor_scalar(gen_scale[:, :], eps[:, :], 1.0, None, ALU.add)
            link(nc.vector.tensor_scalar(own_scale[:, :], eps[:, :], b_ps[:, 0, 0:1], 1.0, ALU.mult, ALU.add))
            dve.wait_ge(base_across, 1)
            for layer in range(2):
                link(nc.vector.tensor_copy(base_all[:, layer * N_WIN:(layer + 1) * N_WIN], b_ps[:, 1, 0:N_WIN]))
            link(nc.vector.tensor_copy(base_all[:, 2 * N_WIN:], b_ps[:, 1, 0:1]))
            general = load_flag(dve)
            dve.wait_ge(gen_mask, 1)

            def build_onehot(w, slot, dst_slot, r):
                nc.vector.tensor_scalar(node_ids[:, :], iota[:, :], base_all[:, bass.ds(w, 1)], None, ALU.add
                                        ).then_inc(ids_ready, 1)
                dve.wait_ge(ids_ready, w + 1)
                dve.wait_ge(dst_loaded[dst_slot], 16 * r + 16)
                nc.vector.tensor_tensor(
                    onehot[:, slot, :, :], dst_idx[:, dst_slot, :].unsqueeze(2).broadcast_to([P, 1 + TILES, P]),
                    node_ids[:, :].unsqueeze(1).broadcast_to([P, 1 + TILES, P]), ALU.is_equal
                    ).then_inc(onehot_built, 1)
                dve.wait_ge(onehot_built, w + 1)

            build_onehot(0, 0, 0, 0)

            for layer in range(2):
                F, FR = F_TAB[layer], F_RES[layer]
                r0 = layer * ROUNDS
                with dve.If(general):
                    with dve.Fori(0, GEN_ROUNDS) as s:
                        dve.wait_ge(gen_own_in, layer * 16 * GEN_ROUNDS + s * 16 + 16)
                        nc.vector.tensor_scalar(z[0:GEN_P, :, 0:F], own[0:GEN_P, :, 0:F], gen_scale[0:GEN_P, layer:layer + 1], None,
                                                ALU.mult).then_inc(gen_scaled, 1)
                    with dve.Fori(0, GEN_TILES) as i:
                        n = i + layer * GEN_TILES
                        dve.wait_ge(gen_dst_in, 16 * n + 16)
                        nc.vector.tensor_copy(gen_dst_f[:, :], gen_dst[:, :]).then_inc(gen_chain, 1)
                        dve.wait_ge(gen_chain, 5 * n + 1)
                        dve.wait_ge(gen_row_in, 16 * n + 16)
                        nc.vector.tensor_scalar(gen_same[:, :], gen_row[:, :], gen_dst_f[:, 0:1], None,
                                                ALU.is_equal).then_inc(gen_matrix, 1)
                        dve.wait_ge(gen_matrix, n + 1)
                        nc.vector.tensor_tensor(gen_before[:, :], gen_same[:, :], earlier[:, :], ALU.mult
                                                ).then_inc(gen_chain, 1)
                        dve.wait_ge(gen_chain, 5 * n + 2)
                        nc.vector.tensor_reduce(out=gen_dup[:, :], in_=gen_before[:, :], axis=AX_X, op=ALU.add
                                                ).then_inc(gen_chain, 1)
                        dve.wait_ge(gen_chain, 5 * n + 3)
                        nc.vector.scalar_tensor_tensor(out=gen_to[:, :], in0=gen_dup[:, :], scalar=float(N_NODES),
                                                       in1=gen_dst_f[:, :], op0=ALU.mult, op1=ALU.add
                                                       ).then_inc(gen_chain, 1)
                        dve.wait_ge(gen_chain, 5 * n + 4)
                        nc.vector.tensor_copy(gen_to_i[:, :], gen_to[:, :]).then_inc(gen_chain, 1)
                        dve.wait_ge(gen_chain, 5 * n + 5)
                        dve.wait_ge(gen_sum_in, 16 * n + 16)
                        dve.wait_ge(gen_summed, n + 1)
                        nc.vector.tensor_tensor(gen_sum[:, 0:F], gen_sum[:, 0:F], b_ps[0:GEN_E, 0, 0:F], ALU.add
                                                ).then_inc(gen_new, 1)
                with dve.Else():
                    dve.nop()

                def window_z(w, j, r, reused=True):
                    dve.wait_ge(groups_summed, groups_after(w))
                    dve.wait_ge(own_loaded, 16 * WINS * (r + 1))
                    if reused:
                        dve.wait_ge(t_ready, blocks_before(2 * r - 1 + j // HALF, layer))
                    nc.vector.scalar_tensor_tensor(out=z[:, j, 0:F], in0=own[:, j, 0:F],
                                                   scalar=own_scale[:, layer:layer + 1],
                                                   in1=sum_ps[:, j % 2, 0:F],
                                                   op0=ALU.mult, op1=ALU.add).then_inc(z_done, 1)

                def result_half(h, j0, resid_at):
                    dve.wait_ge(stored, 16 * (h * HALF - HALF))
                    for j in range(HALF):
                        v = h * HALF + j
                        n = v - N_WIN
                        y = staged[:, j0 + j, 0:FR]
                        dve.wait_ge(b_ready, v + 1)
                        nc.vector.tensor_tensor(y, b_ps[:, j, 0:FR], b2b_s[:, :], ALU.add).then_inc(b_read, 1)
                        dve.wait_ge(b_read, v + 1)
                        dve.wait_ge(resid_loaded, resid_at)
                        nc.vector.tensor_tensor(y, y, resid[:, j0 + j, :], ALU.add).then_inc(ln_chain, 1)
                        dve.wait_ge(ln_chain, 3 * n + 1)
                        nc.vector.bn_stats(out=stats[:, :], in_=y).then_inc(ln_chain, 1)
                        dve.wait_ge(ln_chain, 3 * n + 2)
                        dve.nop(nofuse=True)
                        nc.vector.bn_aggr(out=meanvar[:, j, :], in_=stats[:, :]).then_inc(ln_chain, 1)
                        dve.wait_ge(ln_chain, 3 * n + 3)
                    n = h - 2 * ROUNDS
                    nc.vector.tensor_scalar(var_eps[:, :], meanvar[:, :, 1], LN_EPS, None, ALU.add
                                            ).then_inc(var_ready, 1)
                    dve.wait_ge(std_ready, n + 1)
                    nc.vector.reciprocal(rstd[:, :], std[:, :]).then_inc(rstd_ready, 1)
                    dve.wait_ge(rstd_ready, n + 1)
                    nc.vector.scalar_tensor_tensor(out=shift[:, :], in0=meanvar[:, :, 0], scalar=-1.0, in1=rstd[:, :],
                                                   op0=ALU.mult, op1=ALU.mult).then_inc(shift_ready, 1)
                    dve.wait_ge(shift_ready, n + 1)

                def split_low(w, j):
                    for g in range(SPLIT[layer]):
                        t0, t1 = GROUPS[layer][g]
                        slot = (j % 2) * TILES
                        dve.wait_ge(high_done, split_before(w, layer) + g + 1)
                        form = "p (t f) -> p t f"
                        nc.vector.tensor_tensor(
                            part(low, layer, j, t0, t1).rearrange(form, t=t1 - t0),
                            rows[:, slot + t0:slot + t1, 0:F],
                            part(high, layer, j, t0, t1).bitcast(F32).rearrange(form, t=t1 - t0),
                            ALU.subtract).then_inc(low_done, 1)

                def sums(r, j, reused=True):
                    w = r * WINS + j
                    split_low(w, j)
                    if reused or j:
                        dve.wait_ge(groups_summed, groups_after(w - 1))
                    build_onehot(w + 1, (j + 1) % 2, (j + 1) % WINS, r + (j + 1) // WINS)
                    window_z(w, j, r, reused)

                if layer:
                    dve.wait_ge(weights_in, 16 * 8)
                for j in range(WINS):
                    sums(r0, j, reused=layer == 1)
                if layer:
                    result_half(2 * r0, 0, resid_batches(r0))
                with dve.Fori(r0 + 1, r0 + ROUNDS) as r:
                    sums(r, 0)
                    sums(r, 1)
                    if layer:
                        result_half(2 * r - 1, 2, resid_batches(r))
                    sums(r, 2)
                    sums(r, 3)
                    if layer:
                        result_half(2 * r, 0, resid_batches(r))
                if layer:
                    result_half(2 * (r0 + ROUNDS) - 1, 2, 16 * N_WIN)


_INS = ['x', 'src', 'dst', 'src_tiles', 'dst_tiles', 'L0_gnn_W1a', 'L0_gnn_b1a', 'L0_gnn_W1b', 'L0_gnn_b1b', 'L0_gnn_W2a',
        'L0_gnn_b2a', 'L0_gnn_W2b', 'L0_gnn_b2b', 'L0_gnn_eps1', 'L0_gnn_eps2']


def kernel(**inputs):
    import numpy as _np
    import concourse.bacc as _bacc
    from concourse import mybir as _mybir
    from concourse.bass_utils import run_bass_kernel_spmd as _run

    nc = _bacc.Bacc("TRN2", target_bir_lowering=False, num_devices=1)
    inputs["x"] = _np.concatenate([inputs["x"], _np.zeros((P, F_IN), inputs["x"].dtype)])
    for name, fill in (("src", 0), ("dst", PAD_NODE)):
        inputs[name] = _np.concatenate([inputs[name], _np.full(EDGE_ROOM - N_EDGES, fill, inputs[name].dtype)])
        inputs[name + "_tiles"] = inputs[name].reshape(-1, P).T
    inputs["dst_tiles"] = _np.concatenate([_np.full((P, 1), PAD_NODE, inputs["dst"].dtype), inputs["dst_tiles"]], axis=1)
    arrays, args = {}, []
    for name in _INS:
        a = _np.ascontiguousarray(inputs[name])
        if a.ndim == 0:
            a = a.reshape(1)
        arrays[f"in_{name}"] = a
        args.append(nc.dram_tensor(f"in_{name}", a.shape, _mybir.dt.from_np(a.dtype), kind="ExternalInput").ap())
    out = nc.dram_tensor("out", (N_NODES + P, F_OUT), _mybir.dt.float32, kind="ExternalOutput").ap()
    build(nc, *args, out)
    r = _run(nc, [arrays], core_ids=[0])
    return r.results[0]["out"][:N_NODES]
```
